# Optimizing a Trainium2 kernel written in Bass

```python
import numpy as np
import jax
import jax.numpy as jnp

def _softmax(x, axis=-1):
    return jax.nn.softmax(x, axis=axis)

def _gelu(x):
    return jax.nn.gelu(x, approximate=True)

def _silu(x):
    return jax.nn.silu(x)

def _sigmoid(x):
    return jax.nn.sigmoid(x)

def _layernorm(x, axis=-1, eps=1e-05):
    m = jnp.mean(x, axis=axis, keepdims=True)
    v = jnp.var(x, axis=axis, keepdims=True)
    return (x - m) / jnp.sqrt(v + eps)

def _scatter_add(tgt, idx, src, axis=0):
    return tgt.at[idx].add(src)

def _segment_sum(src, seg, n):
    return jax.ops.segment_sum(src, seg, n)
kernel_name = 'mk_flamingo_gated_d1_seqx_r8_952fff'

def setup_inputs(seed: int=0):
    np.random.seed(seed)
    _w = jnp.asarray

    def _rec_inputs():
        import jax
        import jax.numpy as jnp
        _rk = jax.random.key(seed)
        x = 7.22e-05 + 1 * jax.random.normal(jax.random.fold_in(_rk, 1), (32, 64, 512), jnp.float32)
        _lenS = 64 - jax.random.randint(jax.random.fold_in(_rk, 7), (32,), 0, max(1, 64 // 4) + 1, jnp.int32)
        _lenS2 = 64 - jax.random.randint(jax.random.fold_in(_rk, 8), (32,), 0, max(1, 64 // 4) + 1, jnp.int32)
        _ctx_4096P = jax.random.normal(jax.random.fold_in(_rk, 11), (32, 16, 512), jnp.float32)
        _ctx_4096c = jax.random.dirichlet(jax.random.fold_in(_rk, 511), 0.3 * jnp.ones((16,), jnp.float32), (32, 64))
        _ctx_4096t = jnp.einsum('bsk,bkd->bsd', _ctx_4096c, _ctx_4096P)
        _ctx_4096t = _ctx_4096t * jax.lax.rsqrt(jnp.mean(jnp.square(_ctx_4096t)) + 1e-12) * 0.953939
        ctx_4096 = 4.13588e-05 + 0.999923 * (_ctx_4096t + 0.3 * jax.random.normal(jax.random.fold_in(_rk, 611), (32, 64, 512), jnp.float32))
        _g = jax.random.normal(jax.random.fold_in(_rk, 9001), (2, 1), jnp.float32)
        _g = jnp.sign(_g) * jnp.maximum(jnp.abs(_g), 1.0) + (_g == 0) * 1.0
        g_xattn = _g[0]
        g_ffn = _g[1]
        return (x, ctx_4096, g_xattn, g_ffn)
    x, ctx_4096, g_xattn, g_ffn = _rec_inputs()

    def _L0_xattn_setup():
        import jax, jax.numpy as jnp
        import numpy as np
        B, S, D = (1, 256, 512)
        H, HKV, DK, DV = (32, 8, 128, 128)
        key = jax.random.key(seed)
        ks = jax.random.split(key, 7)
        std = 0.02
        return {'q': jax.random.normal(ks[0], (B, S, D), jnp.float32), 'k': jax.random.normal(ks[1], (B, S, D), jnp.float32), 'v': jax.random.normal(ks[2], (B, S, D), jnp.float32), 'Wq': jax.random.normal(ks[3], (H * DK, D), jnp.float32) * std, 'Wk': jax.random.normal(ks[4], (HKV * DK, D), jnp.float32) * std, 'Wv': jax.random.normal(ks[5], (HKV * DV, D), jnp.float32) * std, 'Wd': jax.random.normal(ks[6], (D, H * DV), jnp.float32) * std}
    _L0_xattn_all = _L0_xattn_setup()
    _L0_xattn_in = {k: v for k, v in _L0_xattn_all.items() if k in ('Wq', 'Wk', 'Wv', 'Wd')}
    del _L0_xattn_all

    def _L0_ffn_setup():
        import jax, jax.numpy as jnp
        import numpy as np
        IN_FEATURES = 512

        def _dequantize(qweight, scale, zero_point):
            N, K_packed = qweight.shape
            groups = K_packed // 3
            p = qweight.reshape(N, groups, 3)
            v0 = p[:, :, 0] & 63
            v1 = p[:, :, 0] >> 6 & 63
            v2 = p[:, :, 1] & 63
            v3 = p[:, :, 2] & 63
            unpacked = jnp.stack([v0, v1, v2, v3], axis=2).reshape(N, groups * 4)
            unpacked = unpacked[:, :IN_FEATURES]
            return (unpacked.astype(jnp.float32) - zero_point) * scale
        key = jax.random.key(seed)
        k1, k2, k3, k4, k5 = jax.random.split(key, 5)
        x = jax.random.normal(k1, (8, 256, 512), dtype=jnp.float32)
        qweight = jax.random.randint(k2, (512, 384), 0, 512, dtype=jnp.int32)
        weight_scale = jax.random.uniform(k3, (512, 1), dtype=jnp.float32) * 0.02 + 0.001
        weight_zero_point = jax.random.uniform(k4, (512, 1), dtype=jnp.float32) * 63.0
        bias = jax.random.normal(k5, (512,), dtype=jnp.float32)
        return {'x': x, 'qweight': qweight, 'weight_scale': weight_scale, 'weight_zero_point': weight_zero_point, 'bias': bias}
    _L0_ffn_all = _L0_ffn_setup()
    _L0_ffn_in = {k: v for k, v in _L0_ffn_all.items() if k in ('qweight', 'weight_scale', 'weight_zero_point', 'bias')}
    del _L0_ffn_all
    return {'x': x, 'ctx_4096': ctx_4096, 'g_xattn': g_xattn, 'g_ffn': g_ffn, 'L0_xattn_Wq': _L0_xattn_in['Wq'], 'L0_xattn_Wk': _L0_xattn_in['Wk'], 'L0_xattn_Wv': _L0_xattn_in['Wv'], 'L0_xattn_Wd': _L0_xattn_in['Wd'], 'L0_ffn_qweight': _L0_ffn_in['qweight'], 'L0_ffn_weight_scale': _L0_ffn_in['weight_scale'], 'L0_ffn_weight_zero_point': _L0_ffn_in['weight_zero_point'], 'L0_ffn_bias': _L0_ffn_in['bias']}

def reference(x, ctx_4096, g_xattn, g_ffn, L0_xattn_Wq, L0_xattn_Wk, L0_xattn_Wv, L0_xattn_Wd, L0_ffn_qweight, L0_ffn_weight_scale, L0_ffn_weight_zero_point, L0_ffn_bias):
    import jax
    import jax.numpy as jnp

    def _L0_xattn_ref(q, k, v, Wq, Wk, Wv, Wd):
        import jax, jax.numpy as jnp
        import numpy as np
        B, S, D = (1, 256, 512)
        H, HKV, DK, DV = (32, 8, 128, 128)
        b, s, _ = q.shape
        exp = H // HKV
        Q = (q @ Wq.T).reshape(b, s, HKV, exp, DK)
        K = (k @ Wk.T).reshape(b, s, HKV, DK)
        V = (v @ Wv.T).reshape(b, s, HKV, DV)
        scale = DK ** (-0.5)
        scores = jnp.einsum('bqhed,bkhd->bheqk', Q, K) * scale
        causal = jnp.tril(jnp.ones((s, s), dtype=bool))
        scores = jnp.where(causal, scores, jnp.finfo(scores.dtype).min)
        probs = jax.nn.softmax(scores, axis=-1)
        attn = jnp.einsum('bheqk,bkhd->bqhed', probs, V)
        attn = attn.reshape(b, s, H * DV)
        return attn @ Wd.T

    def _L0_ffn_ref(x, qweight, weight_scale, weight_zero_point, bias):
        import jax, jax.numpy as jnp
        import numpy as np
        IN_FEATURES = 512

        def _dequantize(qweight, scale, zero_point):
            N, K_packed = qweight.shape
            groups = K_packed // 3
            p = qweight.reshape(N, groups, 3)
            v0 = p[:, :, 0] & 63
            v1 = p[:, :, 0] >> 6 & 63
            v2 = p[:, :, 1] & 63
            v3 = p[:, :, 2] & 63
            unpacked = jnp.stack([v0, v1, v2, v3], axis=2).reshape(N, groups * 4)
            unpacked = unpacked[:, :IN_FEATURES]
            return (unpacked.astype(jnp.float32) - zero_point) * scale
        w = _dequantize(qweight, weight_scale, weight_zero_point)
        return jnp.einsum('bsk,nk->bsn', x, w) + bias
    x = x + jnp.tanh(g_xattn[0]) * _L0_xattn_ref(_layernorm(x, axis=-1), ctx_4096, ctx_4096, L0_xattn_Wq, L0_xattn_Wk, L0_xattn_Wv, L0_xattn_Wd)
    x = x + jnp.tanh(g_ffn[0]) * _L0_ffn_ref(_layernorm(x, axis=-1), L0_ffn_qweight, L0_ffn_weight_scale, L0_ffn_weight_zero_point, L0_ffn_bias)
    return x

_drawn_inputs = setup_inputs


def setup_inputs(seed=0):
    import zlib

    import numpy as np

    out = dict(_drawn_inputs(seed))
    spreads = {}
    factors = {'L0_xattn_Wq': 2.676, 'L0_xattn_Wk': 2.675, 'L0_ffn_weight_zero_point': 8.0}
    for name, (base, spread) in spreads.items():
        noise = np.random.default_rng([zlib.crc32(name.encode()), seed]).standard_normal(out[name].shape)
        drawn = base * np.exp(spread * noise) if base else spread * noise
        out[name] = jnp.asarray(drawn.astype(out[name].dtype))
    for name, factor in factors.items():
        out[name] = (out[name] * factor).astype(out[name].dtype)
    return out
```

```python
from contextlib import ExitStack

import concourse.bass as bass
from concourse import mybir

F32 = mybir.dt.float32
F16 = mybir.dt.float16
I32 = mybir.dt.int32
ALU = mybir.AluOpType
ACT = mybir.ActivationFunctionType
AX = mybir.AxisListType

P = 128
B, S, D = 32, 64, 512
HEADS, GROUPS, DK = 32, 8, 128
HPG = HEADS // GROUPS
KC = D // P
TOKENS = B * S
BT = 512
BLOCKS = TOKENS // BT
TILES = BT // P
BPB = BT // S
PAIRS = HPG // 2
HI, LO = 0, 1
PASSES = ((HI, HI), (HI, LO), (LO, HI))
UNITS = 10

LN_EPS = 1e-5
XN_SCALE = 2.0 ** 8
W_SCALE = 2.0 ** 12
Q_SCALE = 2.0 ** -15
K_SCALE = 2.0 ** -20
P_SCALE = 2.0 ** 10
AV_SCALE = 2.0 ** -10
SCORE_UNSCALE = 1.0 / (XN_SCALE * W_SCALE * Q_SCALE * W_SCALE * W_SCALE * K_SCALE) * DK ** -0.5
Y_UNSCALE = 1.0 / (W_SCALE * W_SCALE * K_SCALE * W_SCALE)
MASKED = -3.0e38
EXPONENT = 0x7F800000
RSQRT_MAGIC = 0x5F3759DF


def build(nc, x, ctxT, wqT, wkT, wvT, wdT, g_x, g_f, qw, w_scale, w_zero, bias, out):
    with ExitStack() as stack:
        def sb(name, shape, dt=F32):
            return stack.enter_context(nc.sbuf_tensor(name, shape, dt))

        def bank(name):
            return stack.enter_context(nc.psum_tensor(name, [P, BT], F32))

        def sem(name):
            return stack.enter_context(nc.semaphore(name))

        xacc = sb("xacc", [P, BLOCKS * TILES, D])
        xT = sb("xT", [P, 2, KC, TOKENS], F16)
        cT = sb("cT", [P, 2, KC, TOKENS], F16)
        raw_q = sb("raw_q", [P, HPG, KC, DK])
        raw_k = sb("raw_k", [P, KC, DK])
        raw_v = sb("raw_v", [P, KC, DK])
        raw_d = sb("raw_d", [P, HPG, D])
        wq = sb("wq", [P, 2, HPG, KC, DK], F16)
        wk = sb("wk", [P, 2, KC, DK], F16)
        wv = sb("wv", [P, 2, KC, DK], F16)
        wd = sb("wd", [P, 2, HPG, D], F16)
        q = sb("q", [P, 2, BPB, HPG, S], F16)
        k = sb("k", [P, 2, BT], F16)
        v_nat = sb("v_nat", [P, TILES, 2, DK], F16)
        v_dup = sb("v_dup", [P, 2, BPB, 2, DK], F16)
        sc = sb("sc", [P, PAIRS, BPB, S])
        pr = sb("pr", [P, PAIRS, BPB, 2, S], F16)
        pT = sb("pT", [P, BPB, HPG, S], F16)
        att = sb("att", [P, 2, HPG, BT], F16)
        shared = sb("shared", [P, 4096])
        c_raw = shared[:, :].rearrange("p (s n) -> p s n", s=2)
        ff_raw = shared[:, 0:1536].bitcast(I32).rearrange("p (c n) -> p c n", c=3)
        ff_w = shared[:, 1536:2560].bitcast(F16).rearrange("p (j n) -> p j n", j=4)
        ff_rows = shared[:, 2560:4096].rearrange("p (r n) -> p r n", r=3)
        ZERO_ROW, SCALE_ROW, BIAS_ROW = range(3)
        xn = sb("xn", [P, 2, D])
        xs = sb("xs", [P, 2, D])
        xh = sb("xh", [P, 2, 2, D], F16)
        ident = sb("ident", [P, P], F16)
        mask = sb("mask", [P, 1, S])
        row_max = sb("row_max", [P, PAIRS, BPB])
        row_sum = sb("row_sum", [P, PAIRS, BPB])
        row_inv = sb("row_inv", [P, PAIRS, BPB])
        gates = sb("gates", [P, 2])
        tg = sb("tg", [P, 2])
        tgy = sb("tgy", [P, 1])
        w_max = sb("w_max", [P, 4])
        w_all = sb("w_all", [P, 4])
        w_grd = sb("w_grd", [P, 4])
        w_pow = sb("w_pow", [P, 4])
        w_inv = sb("w_inv", [P, 4])
        w_mul = sb("w_mul", [P, 4])
        w_prod = sb("w_prod", [P, 2])
        w_now = sb("w_now", [P, 2])
        f_score = sb("f_score", [P, BLOCKS])
        f_y = sb("f_y", [P, BLOCKS])
        c_max = sb("c_max", [P, BLOCKS])
        c_all = sb("c_all", [P, BLOCKS])
        c_grd = sb("c_grd", [P, BLOCKS])
        c_pow = sb("c_pow", [P, BLOCKS])
        c_inv = sb("c_inv", [P, BLOCKS])
        c_mul = sb("c_mul", [P, BLOCKS])
        bn = sb("bn", [P, TILES, 6])
        mv = sb("mv", [P, TILES, 2])
        var_e = sb("var_e", [P, TILES])
        rs = sb("rs", [P, 5, TILES])
        rs_t = sb("rs_t", [P, 2, TILES])
        rstd = sb("rstd", [P, TILES])
        x_sum = sb("x_sum", [P, TILES])

        pa = [bank("pa0"), bank("pa1")]
        py = [bank("py0"), bank("py1")]
        av = [bank("av0"), bank("av1")]
        ps = bank("ps")
        pp = bank("pp")

        x_ld = [sem(f"x_ld{i}") for i in range(BLOCKS)]
        c_ld = [sem(f"c_ld{i}") for i in range(BLOCKS)]
        g_ld = sem("g_ld")
        wqkv_ld = sem("wqkv_ld")
        wd_ld = sem("wd_ld")
        ff_ld = sem("ff_ld")
        v_dup_ld = [sem("v_dup_ld0"), sem("v_dup_ld1")]
        stored = sem("stored")
        const_0 = sem("const_0")
        const_ok = sem("const_ok")
        tanh_ok = sem("tanh_ok")
        tgy_ok = sem("tgy_ok")
        w_max_ok = sem("w_max_ok")
        w_max_seen = sem("w_max_seen")
        w_red_ok = sem("w_red_ok")
        w_grd_ok = sem("w_grd_ok")
        w_pow_ok = sem("w_pow_ok")
        w_inv_ok = sem("w_inv_ok")
        w_mul_ok = sem("w_mul_ok")
        w_prod_ok = sem("w_prod_ok")
        w_now_ok = sem("w_now_ok")
        f_ok = sem("f_ok")
        wq_hi, wq_lo = sem("wq_hi"), sem("wq_lo")
        wk_hi, wk_lo = sem("wk_hi"), sem("wk_lo")
        wv_hi, wv_lo = sem("wv_hi"), sem("wv_lo")
        wd_hi, wd_lo = sem("wd_hi"), sem("wd_lo")
        c_max_ok, c_red_ok, c_grd_ok, c_pow_ok, c_inv_ok, c_mul_ok = [
            sem(s) for s in ("c_max_ok", "c_red_ok", "c_grd_ok", "c_pow_ok", "c_inv_ok", "c_mul_ok")]
        c_hi, c_lo = sem("c_hi"), sem("c_lo")
        bn_ok = sem("bn_ok")
        mv_ok = sem("mv_ok")
        rs_ok = sem("rs_ok")
        xn_ok = sem("xn_ok")
        x_hi, x_lo = sem("x_hi"), sem("x_lo")
        xT_mm = sem("xT_mm")
        xT_ok = sem("xT_ok")
        q_mm, q_hi, q_lo = sem("q_mm"), sem("q_hi"), sem("q_lo")
        k_mm, k_hi, k_lo = sem("k_mm"), sem("k_hi"), sem("k_lo")
        v_mm, v_hi, v_lo = sem("v_mm"), sem("v_hi"), sem("v_lo")
        s_mm = sem("s_mm")
        s_masked = sem("s_masked")
        max_ok = sem("max_ok")
        shifted = sem("shifted")
        exp_ok = sem("exp_ok")
        sum_ok = sem("sum_ok")
        inv_ok = sem("inv_ok")
        norm_ok = sem("norm_ok")
        p_hi, p_lo = sem("p_hi"), sem("p_lo")
        pT_mm, pT_ok = sem("pT_mm"), sem("pT_ok")
        av_mm, av_hi, av_lo = sem("av_mm"), sem("av_hi"), sem("av_lo")
        y_mm, y_ok = sem("y_mm"), sem("y_ok")
        ffw_int, ffw_ok = sem("ffw_int"), sem("ffw_ok")
        row_ok = sem("row_ok")
        f_mm = sem("f_mm")
        f_zero, f_scaled, xb_ok, f_out = sem("f_zero"), sem("f_scaled"), sem("xb_ok"), sem("f_out")

        def wait(eng, s, count):
            if not isinstance(count, int) or count > 0:
                eng.wait_ge(s, count)

        def groups(eng, step):
            for tb in range(BLOCKS):
                step(0, tb, True, False)
            with eng.Fori(1, GROUPS - 1) as g:
                for tb in range(BLOCKS):
                    step(g, tb, False, False)
            for tb in range(BLOCKS):
                step(GROUPS - 1, tb, False, True)

        def following(g, tb):
            return (g, tb + 1, 4 * g + tb + 1) if tb + 1 < BLOCKS else (g + 1, 0, 4 * g + BLOCKS)

        def toks(tb):
            return slice(tb * BT, (tb + 1) * BT)

        block = stack.enter_context(nc.Block())

        @block.sync
        def _(sp):
            def load_x(tb):
                sp.dma_start(xacc[:, tb * TILES:(tb + 1) * TILES, :],
                             x[tb * TILES:(tb + 1) * TILES].rearrange("t p d -> p t d")).then_inc(x_ld[tb], 16)

            def load_ctx(tb):
                wait(sp, c_hi, tb - 1)
                wait(sp, c_lo, tb - 1)
                sp.dma_start(c_raw[:, tb % 2, :], ctxT[tb]).then_inc(c_ld[tb], 16)

            def load_qkv(g):
                sp.dma_start(raw_k[:, :, :], wkT[g].rearrange("p (k n) -> p k n", k=KC)).then_inc(wqkv_ld, 16)
                sp.dma_start(raw_q[:, :, :, :], wqT[g].rearrange("p (h k n) -> p h k n", h=HPG, k=KC)).then_inc(wqkv_ld, 16)
                sp.dma_start(raw_v[:, :, :], wvT[g].rearrange("p (k n) -> p k n", k=KC)).then_inc(wqkv_ld, 16)

            def load_d(g):
                sp.dma_start(raw_d[:, :, :], wdT[g].rearrange("p (h n) -> p h n", h=HPG)).then_inc(wd_ld, 16)

            def duplicate_v(m, par):
                sp.wait_ge(v_hi, m + 1)
                sp.wait_ge(v_lo, m + 1)
                for half in range(2):
                    for src in range(2):
                        sp.dma_start(v_dup[half * S:(half + 1) * S, par, src::2, :, :],
                                     v_nat[src * S:(src + 1) * S, :, :, :]).then_inc(v_dup_ld[par], 16)

            load_x(0)
            load_ctx(0)
            load_qkv(0)
            sp.dma_start(gates[:, 0:1], g_x.partition_broadcast(P)).then_inc(g_ld, 16)
            sp.dma_start(gates[:, 1:2], g_f.partition_broadcast(P)).then_inc(g_ld, 16)
            load_d(0)
            load_x(1)
            load_ctx(1)
            load_x(2)
            load_x(3)
            duplicate_v(0, 0)
            load_ctx(2)

            def step(g, tb, first, last):
                _, tbm, m = following(g, tb)
                if first and tb == 1:
                    load_ctx(3)
                if not last and tb == 0:
                    sp.wait_ge(wq_hi, 4 * (g + 1))
                    sp.wait_ge(wq_lo, 4 * (g + 1))
                    sp.wait_ge(wk_hi, g + 1)
                    sp.wait_ge(wk_lo, g + 1)
                    sp.wait_ge(wv_hi, g + 1)
                    sp.wait_ge(wv_lo, g + 1)
                    load_qkv(g + 1)
                    sp.wait_ge(wd_hi, 4 * (g + 1))
                    sp.wait_ge(wd_lo, 4 * (g + 1))
                    load_d(g + 1)
                if last and tb == 0:
                    sp.wait_ge(c_hi, BLOCKS)
                    sp.wait_ge(c_lo, BLOCKS)
                    sp.dma_start(ff_raw, qw.rearrange("c p n -> p c n")).then_inc(ff_ld, 16)
                    sp.dma_start(ff_rows[:, ZERO_ROW, :], w_zero.partition_broadcast(P)).then_inc(ff_ld, 16)
                    sp.dma_start(ff_rows[:, SCALE_ROW, :], w_scale.partition_broadcast(P)).then_inc(ff_ld, 16)
                    sp.dma_start(ff_rows[:, BIAS_ROW, :], bias.partition_broadcast(P)).then_inc(ff_ld, 16)
                if last and tb > 0:
                    store(tb - 1)
                if not (last and tb == BLOCKS - 1):
                    duplicate_v(m, tbm % 2)

            def store(tb):
                for t in range(tb * TILES, (tb + 1) * TILES):
                    sp.wait_ge(f_out, t + 1)
                    sp.dma_start(out[t], xacc[:, t, :]).then_inc(stored, 16)

            groups(sp, step)
            store(BLOCKS - 1)
            sp.wait_ge(stored, 16 * BLOCKS * TILES)

        @block.gpsimd
        def _(pool):
            pool.memset(ident[:, :], 0.0).then_inc(const_0, 1)
            pool.memset(mask[:, :, :], 0.0).then_inc(const_0, 1)
            pool.wait_ge(const_0, 2)
            pool.affine_select(out=ident[:, :], in_=ident[:, :], compare_op=ALU.not_equal, fill=1.0, base=0,
                               pattern=[[-1, P]], channel_multiplier=1).then_inc(const_ok, 1)
            for half in range(2):
                pool.wait_ge(const_ok, half + 1)
                rows = mask[half * S:(half + 1) * S, 0, :]
                pool.affine_select(out=rows, in_=rows, compare_op=ALU.is_ge, fill=MASKED, base=0,
                                   pattern=[[-1, S]], channel_multiplier=1).then_inc(const_ok, 1)

            def reduce_ctx(tb):
                pool.wait_ge(c_max_ok, tb + 1)
                pool.partition_all_reduce(c_all[:, tb:tb + 1], c_max[:, tb:tb + 1], P,
                                          bass.bass_isa.ReduceOp.max).then_inc(c_red_ok, 1)

            def reduce_w(g):
                pool.wait_ge(w_max_ok, 4 * (g + 1))
                pool.sem_inc(w_max_seen, 1)
                pool.partition_all_reduce(w_all[:, :], w_max[:, :], P,
                                          bass.bass_isa.ReduceOp.max).then_inc(w_red_ok, 1)

            pool.wait_ge(const_ok, 3)
            reduce_ctx(0)
            pool.wait_ge(c_red_ok, 1)
            reduce_w(0)
            pool.wait_ge(w_red_ok, 1)
            reduce_ctx(1)

            def step(g, tb, first, last):
                if first and tb < 2:
                    reduce_ctx(tb + 2)
                if not last and tb == 1:
                    reduce_w(g + 1)
                if last and tb > 0:
                    residual(tb - 1)

            def residual(tb):
                for t in range(tb * TILES, (tb + 1) * TILES):
                    if t == 0:
                        pool.wait_ge(row_ok, 3)
                    pool.wait_ge(xn_ok, BLOCKS * TILES + t + 1)
                    pool.tensor_tensor(xacc[:, t, :], xacc[:, t, :], ff_rows[:, BIAS_ROW, :],
                                       ALU.add).then_inc(xb_ok, 1)

            groups(pool, step)
            residual(BLOCKS - 1)

        @block.scalar
        def _(act):
            def split_ctx(tb):
                act.wait_ge(c_ld[tb], 16)
                act.wait_ge(c_mul_ok, tb + 1)
                act.activation(cT[:, HI, :, toks(tb)], c_raw[:, tb % 2, :].rearrange("p (k n) -> p k n", k=KC),
                               ACT.Copy, scale=c_mul[:, tb:tb + 1]).then_inc(c_hi, 1)

            def split_wq(g, h):
                if h == 0:
                    act.wait_ge(w_mul_ok, g + 1)
                act.activation(wq[:, HI, h, :, :], raw_q[:, h, :, :], ACT.Copy,
                               scale=w_mul[:, 0:1]).then_inc(wq_hi, 1)

            def split_wk(g):
                act.wait_ge(w_mul_ok, g + 1)
                act.activation(wk[:, HI, :, :], raw_k[:, :, :], ACT.Copy, scale=w_mul[:, 1:2]).then_inc(wk_hi, 1)

            def split_wv(g):
                act.activation(wv[:, HI, :, :], raw_v[:, :, :], ACT.Copy, scale=w_mul[:, 2:3]).then_inc(wv_hi, 1)

            def split_wd(g):
                wait(act, y_mm, 16 * g)
                for h in range(HPG):
                    act.activation(wd[:, HI, h, :], raw_d[:, h, :], ACT.Copy, scale=w_mul[:, 3:4]).then_inc(wd_hi, 1)

            def q_part(m, h):
                act.wait_ge(q_mm, 4 * m + h + 1)
                act.activation(q[:, HI, :, h, :], pa[h % 2][:, :].rearrange("p (b s) -> p b s", b=BPB), ACT.Copy,
                               scale=Q_SCALE).then_inc(q_hi, 1)

            def k_part(m):
                act.wait_ge(k_mm, m + 1)
                act.activation(k[:, HI, :], pa[0][:, :], ACT.Copy, scale=K_SCALE).then_inc(k_hi, 1)

            def v_part(m, par):
                act.wait_ge(v_mm, m + 1)
                wait(act, v_dup_ld[1 - par], 32 * (m + par))
                act.activation(v_nat[:, :, HI, :], pa[1][:, :].rearrange("p (t n) -> p t n", t=TILES), ACT.Copy,
                               scale=K_SCALE).then_inc(v_hi, 1)

            def ln_hi(t, summed):
                act.wait_ge(xn_ok, t + 1)
                wait(act, xT_mm, t - 1)
                act.activation(xh[:, t % 2, HI, :], xn[:, t % 2, :], ACT.Copy,
                               accum_out=x_sum[:, t % TILES:t % TILES + 1] if summed else None).then_inc(x_hi, 1)

            def ln_out(t):
                act.wait_ge(xT_mm, t + 1)
                at = t % (BLOCKS * TILES) * P
                act.copy(xT[:, :, :, at:at + P],
                         av[t % 2][:, :].bitcast(F16).rearrange("p (c k n) -> p c k n", c=2, k=KC)).then_inc(xT_ok, 1)

            def exp(n, p):
                act.wait_ge(shifted, 2 * n + p + 1)
                act.activation(sc[:, p, :, :], sc[:, p, :, :], ACT.Exp).then_inc(exp_ok, 1)

            def p_part(n, p):
                act.wait_ge(norm_ok, 2 * n + p + 1)
                act.copy(pr[:, p, :, HI, :], sc[:, p, :, :]).then_inc(p_hi, 1)

            def p_transposed(n, p):
                act.wait_ge(pT_mm, 2 * n + p + 1)
                act.copy(pT[:, :, 2 * p:2 * p + 2, :],
                         pp[:, :].bitcast(F16).rearrange("p (b e s) -> p b e s", b=BPB, e=2)).then_inc(pT_ok, 1)

            def av_part(n, j):
                act.wait_ge(av_mm, 4 * n + j + 1)
                for bb in range(2):
                    at = (2 * j + bb) * S
                    last = act.activation(att[:, HI, :, at:at + S],
                                          av[j % 2][:, bb * 256:(bb + 1) * 256].rearrange("p (h s) -> p h s", h=HPG),
                                          ACT.Copy, scale=AV_SCALE)
                last.then_inc(av_hi, 1)

            def block_tiles(tb, base, summed):
                t0 = base + tb * TILES
                ln_hi(t0, summed)
                for t in range(t0 + 1, t0 + TILES):
                    ln_hi(t, summed)
                    ln_out(t - 1)
                ln_out(t0 + TILES - 1)

            act.wait_ge(g_ld, 32)
            act.activation(tg[:, :], gates[:, :], ACT.Tanh).then_inc(tanh_ok, 1)
            block_tiles(0, 0, False)
            for h in range(HPG):
                split_wq(0, h)
            split_wk(0)
            split_wv(0)
            split_ctx(0)
            for h in range(HPG):
                q_part(0, h)
            k_part(0)
            v_part(0, 0)
            split_ctx(1)
            block_tiles(1, 0, False)

            def step(g, tb, first, last):
                n = 4 * g + tb
                gm, tbm, m = following(g, tb)
                ahead = not (last and tb == BLOCKS - 1)
                if tb == 0:
                    if not first:
                        act.wait_ge(wd_ld, 16 * (g + 1))
                    split_wd(g)
                if ahead:
                    q_part(m, 0)
                    if tb == 2 and not last:
                        split_wq(g + 1, 0)
                exp(n, 0)
                if ahead:
                    q_part(m, 1)
                    if tb == 2 and not last:
                        split_wq(g + 1, 1)
                p_part(n, 0)
                exp(n, 1)
                if ahead:
                    q_part(m, 2)
                    if tb == 2 and not last:
                        split_wq(g + 1, 2)
                if last and tb > 0:
                    block_tiles(tb - 1, BLOCKS * TILES, True)
                p_part(n, 1)
                p_transposed(n, 0)
                if ahead:
                    q_part(m, 3)
                    if tb == 2 and not last:
                        split_wq(g + 1, 3)
                p_transposed(n, 1)
                if ahead:
                    k_part(m)
                    if tb == 2 and not last:
                        split_wk(g + 1)
                av_part(n, 0)
                av_part(n, 1)
                if ahead:
                    v_part(m, tbm % 2)
                    if tb == 2 and not last:
                        split_wv(g + 1)
                av_part(n, 2)
                av_part(n, 3)
                if first and tb < 2:
                    split_ctx(tb + 2)
                    block_tiles(tb + 2, 0, False)

            groups(act, step)
            block_tiles(BLOCKS - 1, BLOCKS * TILES, True)

        @block.vector
        def _(dve):
            def power_of_two(raw, guarded, pow2, inverse, factor, cols, red_ok, grd_ok, pow_ok, inv_ok_, mul_ok, count):
                dve.wait_ge(red_ok, count)
                dve.tensor_scalar(guarded[:, cols], raw[:, cols], 1e-30, None, ALU.max).then_inc(grd_ok, 1)
                dve.wait_ge(grd_ok, count)
                dve.tensor_scalar(pow2[:, cols].bitcast(I32), guarded[:, cols].bitcast(I32), EXPONENT, None,
                                  ALU.bitwise_and).then_inc(pow_ok, 1)
                dve.wait_ge(pow_ok, count)
                dve.reciprocal(inverse[:, cols], pow2[:, cols]).then_inc(inv_ok_, 1)
                dve.wait_ge(inv_ok_, count)
                dve.tensor_scalar(factor[:, cols], inverse[:, cols], W_SCALE, None, ALU.mult).then_inc(mul_ok, 1)

            def ctx_max(tb):
                dve.wait_ge(c_ld[tb], 16)
                dve.tensor_reduce(c_max[:, tb:tb + 1], c_raw[:, tb % 2, :], AX.X, ALU.max,
                                  apply_absolute_value=True).then_inc(c_max_ok, 1)

            def ctx_lo(tb):
                power_of_two(c_all, c_grd, c_pow, c_inv, c_mul, slice(tb, tb + 1),
                             c_red_ok, c_grd_ok, c_pow_ok, c_inv_ok, c_mul_ok, tb + 1)
                dve.wait_ge(c_mul_ok, tb + 1)
                dve.wait_ge(c_hi, tb + 1)
                for kc in range(KC):
                    last = dve.scalar_tensor_tensor(out=cT[:, LO, kc, toks(tb)],
                                                    in0=c_raw[:, tb % 2, kc * BT:(kc + 1) * BT],
                                                    scalar=c_mul[:, tb:tb + 1], in1=cT[:, HI, kc, toks(tb)],
                                                    op0=ALU.mult, op1=ALU.subtract)
                last.then_inc(c_lo, 1)

            def weight_max(g):
                dve.wait_ge(wqkv_ld, 48 * (g + 1))
                for i, raw in enumerate((raw_q[:, :, :, :].rearrange("p h k n -> p (h k n)"),
                                         raw_k[:, :, :].rearrange("p k n -> p (k n)"),
                                         raw_v[:, :, :].rearrange("p k n -> p (k n)"),
                                         raw_d[:, :, :].rearrange("p h n -> p (h n)"))):
                    if i == 3:
                        dve.wait_ge(wd_ld, 16 * (g + 1))
                    dve.tensor_reduce(w_max[:, i:i + 1], raw, AX.X, ALU.max,
                                      apply_absolute_value=True).then_inc(w_max_ok, 1)

            def weight_scale(g):
                power_of_two(w_all, w_grd, w_pow, w_inv, w_mul, slice(0, 4),
                             w_red_ok, w_grd_ok, w_pow_ok, w_inv_ok, w_mul_ok, g + 1)
                for i in range(2):
                    dve.tensor_tensor(w_prod[:, i:i + 1], w_pow[:, 2 * i:2 * i + 1], w_pow[:, 2 * i + 1:2 * i + 2],
                                      ALU.mult).then_inc(w_prod_ok, 1)
                dve.wait_ge(w_mul_ok, g + 1)

            def unscale(g, cols, count):
                if cols.start == 0:
                    dve.wait_ge(w_prod_ok, 2 * (g + 1))
                    dve.tensor_copy(w_now[:, :], w_prod[:, :]).then_inc(w_now_ok, 1)
                    dve.wait_ge(w_now_ok, g + 1)
                dve.tensor_scalar(f_score[:, cols], c_pow[:, cols], w_now[:, 0:1], SCORE_UNSCALE,
                                  ALU.mult, ALU.mult).then_inc(f_ok, 1)
                wait(dve, y_ok, 16 * g)
                dve.tensor_scalar(f_y[:, cols], c_pow[:, cols], w_now[:, 1:2], tgy[:, 0:1],
                                  ALU.mult, ALU.mult).then_inc(f_ok, 1)
                dve.wait_ge(f_ok, count)

            def lo_part(out, in0, scale, hi, done):
                dve.scalar_tensor_tensor(out=out, in0=in0, scalar=scale, in1=hi,
                                         op0=ALU.mult, op1=ALU.subtract).then_inc(done, 1)

            def split_wq(g, h):
                dve.wait_ge(wq_hi, 4 * g + h + 1)
                lo_part(wq[:, LO, h, :, :], raw_q[:, h, :, :], w_mul[:, 0:1], wq[:, HI, h, :, :], wq_lo)

            def split_wk(g):
                dve.wait_ge(wk_hi, g + 1)
                lo_part(wk[:, LO, :, :], raw_k[:, :, :], w_mul[:, 1:2], wk[:, HI, :, :], wk_lo)

            def split_wv(g):
                dve.wait_ge(wv_hi, g + 1)
                lo_part(wv[:, LO, :, :], raw_v[:, :, :], w_mul[:, 2:3], wv[:, HI, :, :], wv_lo)

            def split_wd(g):
                for h in range(HPG):
                    dve.wait_ge(wd_hi, 4 * g + h + 1)
                    lo_part(wd[:, LO, h, :], raw_d[:, h, :], w_mul[:, 3:4], wd[:, HI, h, :], wd_lo)

            def q_part(m, h):
                dve.wait_ge(q_hi, 4 * m + h + 1)
                lo_part(q[:, LO, :, h, :], pa[h % 2][:, :].rearrange("p (b s) -> p b s", b=BPB), Q_SCALE,
                        q[:, HI, :, h, :], q_lo)

            def k_part(m):
                dve.wait_ge(k_hi, m + 1)
                lo_part(k[:, LO, :], pa[0][:, :], K_SCALE, k[:, HI, :], k_lo)

            def v_part(m):
                dve.wait_ge(v_hi, m + 1)
                lo_part(v_nat[:, :, LO, :], pa[1][:, :].rearrange("p (t n) -> p t n", t=TILES), K_SCALE,
                        v_nat[:, :, HI, :], v_lo)

            def scores(n, tb, p):
                dve.wait_ge(s_mm, 2 * n + p + 1)
                dve.scalar_tensor_tensor(out=sc[:, p, :, :], in0=ps[:, :].rearrange("p (b s) -> p b s", b=BPB),
                                         scalar=f_score[:, tb:tb + 1], in1=mask[:, :, :].to_broadcast([P, BPB, S]),
                                         op0=ALU.mult, op1=ALU.add).then_inc(s_masked, 1)
                dve.wait_ge(s_masked, 2 * n + p + 1)
                dve.tensor_reduce(row_max[:, p, :], sc[:, p, :, :], AX.X, ALU.max).then_inc(max_ok, 1)
                dve.wait_ge(max_ok, 2 * n + p + 1)
                dve.tensor_tensor(sc[:, p, :, :], sc[:, p, :, :],
                                  row_max[:, p, :].unsqueeze(2).to_broadcast([P, BPB, S]),
                                  ALU.subtract).then_inc(shifted, 1)

            def normalise(n, p):
                dve.wait_ge(exp_ok, 2 * n + p + 1)
                dve.tensor_reduce(row_sum[:, p, :], sc[:, p, :, :], AX.X, ALU.add).then_inc(sum_ok, 1)
                dve.wait_ge(sum_ok, 2 * n + p + 1)
                dve.reciprocal(row_inv[:, p, :], row_sum[:, p, :]).then_inc(inv_ok, 1)
                dve.wait_ge(inv_ok, 2 * n + p + 1)
                dve.scalar_tensor_tensor(out=sc[:, p, :, :], in0=sc[:, p, :, :], scalar=P_SCALE,
                                         in1=row_inv[:, p, :].unsqueeze(2).to_broadcast([P, BPB, S]),
                                         op0=ALU.mult, op1=ALU.mult).then_inc(norm_ok, 1)

            def p_part(n, p):
                dve.wait_ge(p_hi, 2 * n + p + 1)
                dve.tensor_tensor(pr[:, p, :, LO, :], sc[:, p, :, :], pr[:, p, :, HI, :],
                                  ALU.subtract).then_inc(p_lo, 1)

            def av_part(n, j):
                dve.wait_ge(av_hi, 4 * n + j + 1)
                for bb in range(2):
                    at = (2 * j + bb) * S
                    last = dve.scalar_tensor_tensor(
                        out=att[:, LO, :, at:at + S],
                        in0=av[j % 2][:, bb * 256:(bb + 1) * 256].rearrange("p (h s) -> p h s", h=HPG),
                        scalar=AV_SCALE, in1=att[:, HI, :, at:at + S], op0=ALU.mult, op1=ALU.subtract)
                last.then_inc(av_lo, 1)

            def y_part(n, tb, j):
                dve.wait_ge(y_mm, 4 * n + j + 1)
                t = tb * TILES + j
                dve.scalar_tensor_tensor(out=xacc[:, t, :], in0=py[j % 2][:, :], scalar=f_y[:, tb:tb + 1],
                                         in1=xacc[:, t, :], op0=ALU.mult, op1=ALU.add).then_inc(y_ok, 1)

            def ln_stats(tb, second):
                call = tb + (BLOCKS if second else 0)
                if second:
                    dve.wait_ge(y_ok, 4 * (BLOCKS * (GROUPS - 1) + tb + 1))
                else:
                    dve.wait_ge(x_ld[tb], 16)
                for t in range(TILES):
                    dve.bn_stats(bn[:, t, :], xacc[:, tb * TILES + t, :]).then_inc(bn_ok, 1)
                for t in range(TILES):
                    dve.wait_ge(bn_ok, TILES * call + t + 1)
                    dve.bn_aggr(mv[:, t, :], bn[:, t, :]).then_inc(mv_ok, 1)
                dve.wait_ge(mv_ok, TILES * (call + 1))
                count = 13 * call

                def chained(ins):
                    nonlocal count
                    count += 1
                    ins.then_inc(rs_ok, 1)
                    dve.wait_ge(rs_ok, count)

                chained(dve.tensor_scalar(var_e[:, :], mv[:, :, 1], LN_EPS, None, ALU.add))
                chained(dve.tensor_scalar(rs[:, 4, :].bitcast(I32), var_e[:, :].bitcast(I32), 1, None,
                                          ALU.logical_shift_right))
                chained(dve.tensor_scalar(rs[:, 0, :].bitcast(I32), rs[:, 4, :].bitcast(I32), -1.0, float(RSQRT_MAGIC),
                                          ALU.mult, ALU.add))
                for i in range(3):
                    y = rs[:, i, :]
                    chained(dve.tensor_tensor(rs_t[:, 0, :], y, y, ALU.mult))
                    chained(dve.scalar_tensor_tensor(out=rs_t[:, 1, :], in0=rs_t[:, 0, :], scalar=-0.5, in1=var_e[:, :],
                                                     op0=ALU.mult, op1=ALU.mult))
                    chained(dve.scalar_tensor_tensor(out=rs[:, i + 1, :], in0=rs_t[:, 1, :], scalar=1.5, in1=y,
                                                     op0=ALU.add, op1=ALU.mult))
                chained(dve.tensor_scalar(rstd[:, :], rs[:, 3, :], XN_SCALE, None, ALU.mult))

            def ln_tile(t):
                wait(dve, x_hi, t - 1)
                at = t % TILES
                dve.tensor_scalar(xn[:, t % 2, :], xacc[:, t % (BLOCKS * TILES), :], mv[:, at, 0:1], rstd[:, at:at + 1],
                                  ALU.subtract, ALU.mult).then_inc(xn_ok, 1)
                dve.wait_ge(xn_ok, t + 1)
                dve.wait_ge(x_hi, t + 1)
                dve.tensor_tensor(xh[:, t % 2, LO, :], xn[:, t % 2, :], xh[:, t % 2, HI, :],
                                  ALU.subtract).then_inc(x_lo, 1)

            def ffn_weights():
                dve.wait_ge(ff_ld, 64)
                for j, (word, shift) in enumerate(((0, 0), (0, 6), (1, 0), (2, 0))):
                    dve.tensor_scalar(xn[:, j % 2, :].bitcast(I32), ff_raw[:, word, :], shift, 63,
                                      ALU.logical_shift_right, ALU.bitwise_and).then_inc(ffw_int, 1)
                    dve.wait_ge(ffw_int, j + 1)
                    dve.tensor_copy(ff_w[:, j, :], xn[:, j % 2, :].bitcast(I32)).then_inc(ffw_ok, 1)
                dve.tensor_scalar(ff_rows[:, ZERO_ROW, :], ff_rows[:, ZERO_ROW, :], -1.0, None,
                                  ALU.mult).then_inc(row_ok, 1)
                dve.tensor_scalar(ff_rows[:, SCALE_ROW, :], ff_rows[:, SCALE_ROW, :], tg[:, 1:2], 1.0 / XN_SCALE,
                                  ALU.mult, ALU.mult).then_inc(row_ok, 1)
                dve.tensor_scalar(ff_rows[:, BIAS_ROW, :], ff_rows[:, BIAS_ROW, :], tg[:, 1:2], None,
                                  ALU.mult).then_inc(row_ok, 1)

            def ffn_out(t):
                dve.wait_ge(f_mm, t + 1)
                dve.scalar_tensor_tensor(out=xs[:, t % 2, :], in0=ff_rows[:, ZERO_ROW, :],
                                         scalar=x_sum[:, t % TILES:t % TILES + 1],
                                         in1=py[t % 2][:, :], op0=ALU.mult, op1=ALU.add).then_inc(f_zero, 1)
                dve.wait_ge(f_zero, t + 1)
                dve.tensor_tensor(xs[:, t % 2, :], xs[:, t % 2, :], ff_rows[:, SCALE_ROW, :],
                                  ALU.mult).then_inc(f_scaled, 1)
                dve.wait_ge(f_scaled, t + 1)
                dve.wait_ge(xb_ok, t + 1)
                dve.tensor_tensor(xacc[:, t, :], xacc[:, t, :], xs[:, t % 2, :], ALU.add).then_inc(f_out, 1)

            ln_stats(0, False)
            for t in range(TILES):
                ln_tile(t)
            ctx_max(0)
            weight_max(0)
            weight_scale(0)
            for h in range(HPG):
                split_wq(0, h)
            split_wk(0)
            split_wv(0)
            ctx_lo(0)
            dve.wait_ge(tanh_ok, 1)
            dve.tensor_scalar(tgy[:, :], tg[:, 0:1], Y_UNSCALE, None, ALU.mult).then_inc(tgy_ok, 1)
            dve.wait_ge(tgy_ok, 1)
            ctx_max(1)
            for h in range(HPG):
                q_part(0, h)
            k_part(0)
            v_part(0)
            ctx_lo(1)
            ln_stats(1, False)
            for t in range(TILES, 2 * TILES):
                ln_tile(t)

            def step(g, tb, first, last):
                n = 4 * g + tb
                gm, tbm, m = following(g, tb)
                ahead = not (last and tb == BLOCKS - 1)
                reweigh = tb == 2 and not last
                if first:
                    if tb == 0:
                        dve.wait_ge(const_ok, 3)
                    unscale(g, slice(tb, tb + 1), 2 * (tb + 1))
                elif tb == 0:
                    unscale(g, slice(0, BLOCKS), 2 * BLOCKS + 2 * g)
                scores(n, tb, 0)
                if ahead:
                    q_part(m, 0)
                    if reweigh:
                        split_wq(g + 1, 0)
                scores(n, tb, 1)
                normalise(n, 0)
                if ahead:
                    q_part(m, 1)
                    if reweigh:
                        split_wq(g + 1, 1)
                p_part(n, 0)
                if last and tb > 0:
                    ln_stats(tb - 1, True)
                    for t in range(2):
                        ln_tile((BLOCKS + tb - 1) * TILES + t)
                normalise(n, 1)
                if ahead:
                    q_part(m, 2)
                    if reweigh:
                        split_wq(g + 1, 2)
                if last and tb > 0:
                    for t in range(2, TILES):
                        ln_tile((BLOCKS + tb - 1) * TILES + t)
                p_part(n, 1)
                if ahead:
                    q_part(m, 3)
                    if reweigh:
                        split_wq(g + 1, 3)
                    k_part(m)
                    if reweigh:
                        split_wk(g + 1)
                if tb == 0:
                    split_wd(g)
                if tb == 1 and not last:
                    weight_max(g + 1)
                if first and tb < 2:
                    ctx_max(tb + 2)
                av_part(n, 0)
                av_part(n, 1)
                if ahead:
                    v_part(m)
                    if reweigh:
                        split_wv(g + 1)
                if tb == 1 and not last:
                    weight_scale(g + 1)
                if last and tb == 0:
                    ffn_weights()
                av_part(n, 2)
                av_part(n, 3)
                if first and tb < 2:
                    ctx_lo(tb + 2)
                    ln_stats(tb + 2, False)
                if last and tb > 0:
                    for t in range(TILES):
                        ffn_out((tb - 1) * TILES + t)
                for j in range(TILES):
                    if first and tb < 2:
                        ln_tile((tb + 2) * TILES + j)
                    y_part(n, tb, j)

            groups(dve, step)
            ln_stats(BLOCKS - 1, True)
            for t in range(TILES):
                ln_tile((2 * BLOCKS - 1) * TILES + t)
            for t in range(TILES):
                ffn_out((BLOCKS - 1) * TILES + t)

        @block.tensor
        def _(pe):
            def product(out, stationary, moving, count):
                for i in range(count):
                    for a, b in PASSES:
                        last = pe.matmul(out, stationary(a, i), moving(b, i),
                                         start=(i == 0 and (a, b) == PASSES[0]),
                                         stop=(i == count - 1 and (a, b) == PASSES[-1]))
                return last

            def q_unit(gm, tbm, m, h, in_first):
                pe.wait_ge(wq_hi, 4 * gm + h + 1)
                pe.wait_ge(wq_lo, 4 * gm + h + 1)
                if h == 0:
                    if in_first:
                        pe.wait_ge(xT_ok, TILES * (tbm + 1))
                    wait(pe, k_hi, m)
                    wait(pe, k_lo, m)
                elif h == 1:
                    wait(pe, v_hi, m)
                    wait(pe, v_lo, m)
                else:
                    pe.wait_ge(q_hi, 4 * m + h - 1)
                    pe.wait_ge(q_lo, 4 * m + h - 1)
                product(pa[h % 2][:, :], lambda a, i: wq[:, a, h, i, :], lambda b, i: xT[:, b, i, toks(tbm)],
                        KC).then_inc(q_mm, 1)

            def k_unit(gm, tbm, m, in_first):
                pe.wait_ge(wk_hi, gm + 1)
                pe.wait_ge(wk_lo, gm + 1)
                if in_first:
                    pe.wait_ge(c_hi, tbm + 1)
                    pe.wait_ge(c_lo, tbm + 1)
                pe.wait_ge(q_hi, 4 * m + 3)
                pe.wait_ge(q_lo, 4 * m + 3)
                product(pa[0][:, :], lambda a, i: wk[:, a, i, :], lambda b, i: cT[:, b, i, toks(tbm)],
                        KC).then_inc(k_mm, 1)

            def v_unit(gm, tbm, m):
                pe.wait_ge(wv_hi, gm + 1)
                pe.wait_ge(wv_lo, gm + 1)
                pe.wait_ge(q_hi, 4 * m + 4)
                pe.wait_ge(q_lo, 4 * m + 4)
                for t in range(TILES):
                    at = tbm * BT + t * P
                    last = product(pa[1][:, t * P:(t + 1) * P], lambda a, i: cT[:, a, i, at:at + P],
                                   lambda b, i: wv[:, b, i, :], KC)
                last.then_inc(v_mm, 1)

            def score_unit(n, p):
                pe.wait_ge(q_hi, 4 * n + 2 * p + 2)
                pe.wait_ge(q_lo, 4 * n + 2 * p + 2)
                if p == 0:
                    pe.wait_ge(k_hi, n + 1)
                    pe.wait_ge(k_lo, n + 1)
                wait(pe, s_masked, 2 * n + p)
                for b in range(BPB):
                    for a, c in PASSES:
                        last = pe.matmul(ps[:, b * S:(b + 1) * S],
                                         q[:, a, b, 2 * p:2 * p + 2, :].rearrange("p e s -> p (e s)"),
                                         k[:, c, b * S:(b + 1) * S],
                                         start=((a, c) == PASSES[0]), stop=((a, c) == PASSES[-1]))
                last.then_inc(s_mm, 1)

            def p_transpose(n, p):
                pe.wait_ge(p_hi, 2 * n + p + 1)
                pe.wait_ge(p_lo, 2 * n + p + 1)
                wait(pe, pT_ok, 2 * n + p)
                bank16 = pp[:, :].bitcast(F16)
                for b in range(BPB):
                    last = pe.transpose(bank16[:, b * P:(b + 1) * P],
                                        pr[:, p, b, :, :].rearrange("p c s -> p (c s)"), ident[:, :])
                last.then_inc(pT_mm, 1)

            def av_unit(n, par, j):
                if j == 0:
                    pe.wait_ge(pT_ok, 2 * n + 2)
                    pe.wait_ge(v_dup_ld[par], 32 * (n + 2 - par))
                wait(pe, av_hi, 4 * n + j - 1)
                wait(pe, av_lo, 4 * n + j - 1)
                for bb in range(2):
                    b = 2 * j + bb
                    for c in (HI, LO):
                        last = pe.matmul(av[j % 2][:, bb * 256:(bb + 1) * 256], v_dup[:, par, b, c, :],
                                         pT[:, b, :, :].rearrange("p h s -> p (h s)"),
                                         start=(c == HI), stop=(c == LO))
                last.then_inc(av_mm, 1)

            def y_unit(g, n, j):
                if j == 0:
                    pe.wait_ge(wd_hi, 4 * (g + 1))
                    pe.wait_ge(wd_lo, 4 * (g + 1))
                pe.wait_ge(av_hi, 4 * n + j + 1)
                pe.wait_ge(av_lo, 4 * n + j + 1)
                wait(pe, y_ok, 4 * n + j - 1)
                product(py[j % 2][:, :], lambda a, h: att[:, a, h, j * P:(j + 1) * P],
                        lambda b, h: wd[:, b, h, :], HPG).then_inc(y_mm, 1)

            def ln_transpose(t, av_before):
                pe.wait_ge(x_hi, t + 1)
                pe.wait_ge(x_lo, t + 1)
                wait(pe, xT_ok, t - 1)
                wait(pe, av_hi, av_before)
                wait(pe, av_lo, av_before)
                bank16 = av[t % 2][:, :].bitcast(F16)
                for c in (HI, LO):
                    for i in range(KC):
                        if t < BLOCKS * TILES:
                            part = xh[:, t % 2, c, i * P:(i + 1) * P]
                        else:
                            part = xh[:, t % 2, c, :].rearrange("p (i j) -> p j i", j=KC)[:, i, :]
                        at = (c * KC + i) * P
                        last = pe.transpose(bank16[:, at:at + P], part, ident[:, :])
                last.then_inc(xT_mm, 1)

            def ffn_unit(t, y_before):
                if t == 0:
                    pe.wait_ge(ffw_ok, 4)
                pe.wait_ge(xT_ok, BLOCKS * TILES + t + 1)
                if t % TILES < 2:
                    pe.wait_ge(y_ok, y_before)
                else:
                    pe.wait_ge(f_zero, t - 1)
                for i in range(KC):
                    for a in (HI, LO):
                        last = pe.matmul(py[t % 2][:, :], xT[:, a, i, t * P:(t + 1) * P], ff_w[:, i, :],
                                         start=(i == 0 and a == HI), stop=(i == KC - 1 and a == LO))
                last.then_inc(f_mm, 1)

            pe.wait_ge(const_ok, 1)
            for t in range(TILES):
                ln_transpose(t, 0)
            for h in range(HPG):
                q_unit(0, 0, 0, h, True)
            k_unit(0, 0, 0, True)
            v_unit(0, 0, 0)
            for t in range(TILES, 2 * TILES):
                ln_transpose(t, 0)

            def step(g, tb, first, last):
                n = 4 * g + tb
                gm, tbm, m = following(g, tb)
                ahead = not (last and tb == BLOCKS - 1)
                in_first = first and tbm > 0
                score_unit(n, 0)
                if ahead:
                    q_unit(gm, tbm, m, 0, in_first)
                score_unit(n, 1)
                if ahead:
                    q_unit(gm, tbm, m, 1, in_first)
                    q_unit(gm, tbm, m, 2, in_first)
                if last and tb > 0:
                    for t in range(TILES):
                        ln_transpose((BLOCKS + tb - 1) * TILES + t, 4 * n)
                p_transpose(n, 0)
                if ahead:
                    q_unit(gm, tbm, m, 3, in_first)
                p_transpose(n, 1)
                if ahead:
                    k_unit(gm, tbm, m, in_first)
                if first and tb > 0 and tb < 3:
                    pe.wait_ge(xT_ok, (tb + 2) * TILES)
                elif first and tb == 0:
                    pe.wait_ge(xT_ok, 2 * TILES)
                elif last and tb > 0:
                    pe.wait_ge(xT_ok, (BLOCKS + tb) * TILES)
                av_unit(n, tb % 2, 0)
                av_unit(n, tb % 2, 1)
                if ahead:
                    v_unit(gm, tbm, m)
                av_unit(n, tb % 2, 2)
                av_unit(n, tb % 2, 3)
                if last and tb > 0:
                    for t in range(TILES):
                        ffn_unit((tb - 1) * TILES + t, 4 * n)
                    pe.wait_ge(f_zero, tb * TILES)
                y_unit(g, n, 0)
                y_unit(g, n, 1)
                if first and tb < 2:
                    ln_transpose((tb + 2) * TILES, 4 * n + 4)
                y_unit(g, n, 2)
                if first and tb < 2:
                    ln_transpose((tb + 2) * TILES + 1, 4 * n + 4)
                y_unit(g, n, 3)
                if first and tb < 2:
                    ln_transpose((tb + 2) * TILES + 2, 4 * n + 4)
                    ln_transpose((tb + 2) * TILES + 3, 4 * n + 4)

            groups(pe, step)
            for t in range(TILES):
                ln_transpose((2 * BLOCKS - 1) * TILES + t, 4 * BLOCKS * GROUPS)
            for t in range((BLOCKS - 1) * TILES, BLOCKS * TILES):
                ffn_unit(t, 4 * BLOCKS * GROUPS)


def kernel(**inputs):
    import numpy as np
    import concourse.bacc as bacc
    from concourse.bass_utils import run_bass_kernel_spmd

    a = {name: np.asarray(v) for name, v in inputs.items()}
    laid = {
        "x": a["x"].reshape(BLOCKS * TILES, P, D),
        "ctxT": a["ctx_4096"].reshape(BLOCKS, BT, KC, P).transpose(0, 3, 2, 1).reshape(BLOCKS, P, KC * BT),
        "wqT": a["L0_xattn_Wq"].reshape(GROUPS, HPG, DK, KC, P).transpose(0, 4, 1, 3, 2).reshape(GROUPS, P, HPG * KC * DK),
        "wkT": a["L0_xattn_Wk"].reshape(GROUPS, DK, KC, P).transpose(0, 3, 2, 1).reshape(GROUPS, P, KC * DK),
        "wvT": a["L0_xattn_Wv"].reshape(GROUPS, DK, KC, P).transpose(0, 3, 2, 1).reshape(GROUPS, P, KC * DK),
        "wdT": a["L0_xattn_Wd"].reshape(D, GROUPS, HPG, DK).transpose(1, 3, 2, 0).reshape(GROUPS, DK, HPG * D),
        "g_x": a["g_xattn"].reshape(1),
        "g_f": a["g_ffn"].reshape(1),
        "qw": a["L0_ffn_qweight"].reshape(D, P, 3).transpose(2, 1, 0),
        "w_scale": a["L0_ffn_weight_scale"].reshape(D),
        "w_zero": a["L0_ffn_weight_zero_point"].reshape(D),
        "bias": a["L0_ffn_bias"].reshape(D),
    }
    laid = {name: np.ascontiguousarray(v) for name, v in laid.items()}
    nc = bacc.Bacc("TRN2", target_bir_lowering=False, num_devices=1)
    args = [nc.dram_tensor(f"in_{name}", v.shape, mybir.dt.from_np(v.dtype), kind="ExternalInput").ap()
            for name, v in laid.items()]
    result = nc.dram_tensor("out_x", (BLOCKS * TILES, P, D), F32, kind="ExternalOutput").ap()
    build(nc, *args, result)
    r = run_bass_kernel_spmd(nc, [{f"in_{name}": v for name, v in laid.items()}], core_ids=[0])
    return r.results[0]["out_x"].reshape(B, S, D)
```

```python
from contextlib import ExitStack

import concourse.bass as bass
from concourse import mybir

F32 = mybir.dt.float32
F16 = mybir.dt.float16
I32 = mybir.dt.int32
ALU = mybir.AluOpType
ACT = mybir.ActivationFunctionType
AX = mybir.AxisListType

P = 128
B, S, D = 32, 64, 512
HEADS, GROUPS, DK = 32, 8, 128
HPG = HEADS // GROUPS
KC = D // P
TOKENS = B * S
BT = 512
BLOCKS = TOKENS // BT
TILES = BT // P
BPB = BT // S
PAIRS = HPG // 2
HI, LO = 0, 1
PASSES = ((HI, HI), (HI, LO), (LO, HI))
UNITS = 10

LN_EPS = 1e-5
XN_SCALE = 2.0 ** 8
W_SCALE = 2.0 ** 12
Q_SCALE = 2.0 ** -15
K_SCALE = 2.0 ** -20
P_SCALE = 2.0 ** 10
AV_SCALE = 2.0 ** -10
SCORE_UNSCALE = 1.0 / (XN_SCALE * W_SCALE * Q_SCALE * W_SCALE * W_SCALE * K_SCALE) * DK ** -0.5
Y_UNSCALE = 1.0 / (W_SCALE * W_SCALE * K_SCALE * W_SCALE)
MASKED = -3.0e38
EXPONENT = 0x7F800000
RSQRT_MAGIC = 0x5F3759DF


def build(nc, x, ctxT, wqT, wkT, wvT, wdT, g_x, g_f, qw, w_scale, w_zero, bias, out):
    with ExitStack() as stack:
        def sb(name, shape, dt=F32):
            return stack.enter_context(nc.sbuf_tensor(name, shape, dt))

        def bank(name):
            return stack.enter_context(nc.psum_tensor(name, [P, BT], F32))

        def sem(name):
            return stack.enter_context(nc.semaphore(name))

        xacc = sb("xacc", [P, BLOCKS * TILES, D])
        xT = sb("xT", [P, 2, KC, TOKENS], F16)
        cT = sb("cT", [P, 2, KC, TOKENS], F16)
        raw_q = sb("raw_q", [P, HPG, KC, DK])
        raw_k = sb("raw_k", [P, KC, DK])
        raw_v = sb("raw_v", [P, KC, DK])
        raw_d = sb("raw_d", [P, HPG, D])
        wq = sb("wq", [P, 2, HPG, KC, DK], F16)
        wk = sb("wk", [P, 2, KC, DK], F16)
        wv = sb("wv", [P, 2, KC, DK], F16)
        wd = sb("wd", [P, 2, HPG, D], F16)
        q = sb("q", [P, 2, BPB, HPG, S], F16)
        k = sb("k", [P, 2, BT], F16)
        v_nat = sb("v_nat", [P, TILES, 2, DK], F16)
        v_dup = sb("v_dup", [P, 2, BPB, 2, DK], F16)
        sc = sb("sc", [P, PAIRS, BPB, S])
        pr = sb("pr", [P, PAIRS, BPB, 2, S], F16)
        pT = sb("pT", [P, BPB, HPG, S], F16)
        att = sb("att", [P, 2, HPG, BT], F16)
        shared = sb("shared", [P, 4096])
        c_raw = shared[:, :].rearrange("p (s n) -> p s n", s=2)
        ff_raw = shared[:, 0:1536].bitcast(I32).rearrange("p (c n) -> p c n", c=3)
        ff_w = shared[:, 1536:2560].bitcast(F16).rearrange("p (j n) -> p j n", j=4)
        ff_rows = shared[:, 2560:4096].rearrange("p (r n) -> p r n", r=3)
        ZERO_ROW, SCALE_ROW, BIAS_ROW = range(3)
        xn = sb("xn", [P, 2, D])
        xs = sb("xs", [P, 2, D])
        xh = sb("xh", [P, 2, 2, D], F16)
        ident = sb("ident", [P, P], F16)
        mask = sb("mask", [P, 1, S])
        row_max = sb("row_max", [P, PAIRS, BPB])
        row_sum = sb("row_sum", [P, PAIRS, BPB])
        row_inv = sb("row_inv", [P, PAIRS, BPB])
        gates = sb("gates", [P, 2])
        tg = sb("tg", [P, 2])
        tgy = sb("tgy", [P, 1])
        w_max = sb("w_max", [P, 4])
        w_all = sb("w_all", [P, 4])
        w_grd = sb("w_grd", [P, 4])
        w_pow = sb("w_pow", [P, 4])
        w_inv = sb("w_inv", [P, 4])
        w_mul = sb("w_mul", [P, 4])
        w_prod = sb("w_prod", [P, 2])
        w_now = sb("w_now", [P, 2])
        f_score = sb("f_score", [P, BLOCKS])
        f_y = sb("f_y", [P, BLOCKS])
        c_max = sb("c_max", [P, BLOCKS])
        c_all = sb("c_all", [P, BLOCKS])
        c_grd = sb("c_grd", [P, BLOCKS])
        c_pow = sb("c_pow", [P, BLOCKS])
        c_inv = sb("c_inv", [P, BLOCKS])
        c_mul = sb("c_mul", [P, BLOCKS])
        bn = sb("bn", [P, TILES, 6])
        mv = sb("mv", [P, TILES, 2])
        var_e = sb("var_e", [P, TILES])
        rs = sb("rs", [P, 5, TILES])
        rs_t = sb("rs_t", [P, 2, TILES])
        rstd = sb("rstd", [P, TILES])
        x_sum = sb("x_sum", [P, BLOCKS * TILES])

        pa = [bank("pa0"), bank("pa1")]
        py = [bank("py0"), bank("py1")]
        av = [bank("av0"), bank("av1")]
        ps = bank("ps")
        pp = bank("pp")

        x_ld = [sem(f"x_ld{i}") for i in range(BLOCKS)]
        c_ld = [sem(f"c_ld{i}") for i in range(BLOCKS)]
        g_ld = sem("g_ld")
        wqkv_ld = sem("wqkv_ld")
        wd_ld = sem("wd_ld")
        ff_ld = sem("ff_ld")
        v_dup_ld = [sem("v_dup_ld0"), sem("v_dup_ld1")]
        stored = sem("stored")
        const_0 = sem("const_0")
        const_ok = sem("const_ok")
        tanh_ok = sem("tanh_ok")
        tgy_ok = sem("tgy_ok")
        w_max_ok = sem("w_max_ok")
        w_max_seen = sem("w_max_seen")
        w_red_ok = sem("w_red_ok")
        w_grd_ok = sem("w_grd_ok")
        w_pow_ok = sem("w_pow_ok")
        w_inv_ok = sem("w_inv_ok")
        w_mul_ok = sem("w_mul_ok")
        w_prod_ok = sem("w_prod_ok")
        w_now_ok = sem("w_now_ok")
        f_ok = sem("f_ok")
        wq_hi, wq_lo = sem("wq_hi"), sem("wq_lo")
        wk_hi, wk_lo = sem("wk_hi"), sem("wk_lo")
        wv_hi, wv_lo = sem("wv_hi"), sem("wv_lo")
        wd_hi, wd_lo = sem("wd_hi"), sem("wd_lo")
        c_max_ok, c_red_ok, c_grd_ok, c_pow_ok, c_inv_ok, c_mul_ok = [
            sem(s) for s in ("c_max_ok", "c_red_ok", "c_grd_ok", "c_pow_ok", "c_inv_ok", "c_mul_ok")]
        c_hi, c_lo = sem("c_hi"), sem("c_lo")
        bn_ok = sem("bn_ok")
        mv_ok = sem("mv_ok")
        rs_ok = sem("rs_ok")
        xn_ok = sem("xn_ok")
        x_hi, x_lo = sem("x_hi"), sem("x_lo")
        xT_mm = sem("xT_mm")
        xT_ok = sem("xT_ok")
        q_mm, q_hi, q_lo = sem("q_mm"), sem("q_hi"), sem("q_lo")
        k_mm, k_hi, k_lo = sem("k_mm"), sem("k_hi"), sem("k_lo")
        v_mm, v_hi, v_lo = sem("v_mm"), sem("v_hi"), sem("v_lo")
        s_mm = sem("s_mm")
        s_masked = sem("s_masked")
        max_ok = sem("max_ok")
        shifted = sem("shifted")
        exp_ok = sem("exp_ok")
        sum_ok = sem("sum_ok")
        inv_ok = sem("inv_ok")
        norm_ok = sem("norm_ok")
        p_hi, p_lo = sem("p_hi"), sem("p_lo")
        pT_mm, pT_ok = sem("pT_mm"), sem("pT_ok")
        av_mm, av_hi, av_lo = sem("av_mm"), sem("av_hi"), sem("av_lo")
        y_mm, y_ok = sem("y_mm"), sem("y_ok")
        ffw_int, ffw_ok = sem("ffw_int"), sem("ffw_ok")
        row_ok = sem("row_ok")
        f_mm = sem("f_mm")
        f_zero, f_scaled, xb_ok, f_out = sem("f_zero"), sem("f_scaled"), sem("xb_ok"), sem("f_out")

        def wait(eng, s, count):
            if not isinstance(count, int) or count > 0:
                eng.wait_ge(s, count)

        def groups(eng, step):
            for tb in range(BLOCKS):
                step(0, tb, True, False)
            with eng.Fori(1, GROUPS - 1) as g:
                for tb in range(BLOCKS):
                    step(g, tb, False, False)
            for tb in range(BLOCKS):
                step(GROUPS - 1, tb, False, True)

        def following(g, tb):
            return (g, tb + 1, 4 * g + tb + 1) if tb + 1 < BLOCKS else (g + 1, 0, 4 * g + BLOCKS)

        def toks(tb):
            return slice(tb * BT, (tb + 1) * BT)

        block = stack.enter_context(nc.Block())

        @block.sync
        def _(sp):
            def load_x(tb):
                sp.dma_start(xacc[:, tb * TILES:(tb + 1) * TILES, :],
                             x[tb * TILES:(tb + 1) * TILES].rearrange("t p d -> p t d")).then_inc(x_ld[tb], 16)

            def load_ctx(tb):
                wait(sp, c_hi, tb - 1)
                wait(sp, c_lo, tb - 1)
                sp.dma_start(c_raw[:, tb % 2, :], ctxT[tb]).then_inc(c_ld[tb], 16)

            def load_qkv(g):
                sp.dma_start(raw_k[:, :, :], wkT[g].rearrange("p (k n) -> p k n", k=KC)).then_inc(wqkv_ld, 16)
                sp.dma_start(raw_q[:, :, :, :], wqT[g].rearrange("p (h k n) -> p h k n", h=HPG, k=KC)).then_inc(wqkv_ld, 16)
                sp.dma_start(raw_v[:, :, :], wvT[g].rearrange("p (k n) -> p k n", k=KC)).then_inc(wqkv_ld, 16)

            def load_d(g):
                sp.dma_start(raw_d[:, :, :], wdT[g].rearrange("p (h n) -> p h n", h=HPG)).then_inc(wd_ld, 16)

            def duplicate_v(m, par):
                sp.wait_ge(v_hi, m + 1)
                sp.wait_ge(v_lo, m + 1)
                for half in range(2):
                    for src in range(2):
                        sp.dma_start(v_dup[half * S:(half + 1) * S, par, src::2, :, :],
                                     v_nat[src * S:(src + 1) * S, :, :, :]).then_inc(v_dup_ld[par], 16)

            load_x(0)
            load_qkv(0)
            load_d(0)
            sp.dma_start(gates[:, 0:1], g_x.partition_broadcast(P)).then_inc(g_ld, 16)
            sp.dma_start(gates[:, 1:2], g_f.partition_broadcast(P)).then_inc(g_ld, 16)
            load_ctx(0)
            load_x(1)
            load_ctx(1)
            load_x(2)
            load_x(3)
            duplicate_v(0, 0)
            load_ctx(2)

            def step(g, tb, first, last):
                _, tbm, m = following(g, tb)
                if first and tb == 1:
                    load_ctx(3)
                if not last and tb == 0:
                    sp.wait_ge(wq_hi, 4 * (g + 1))
                    sp.wait_ge(wq_lo, 4 * (g + 1))
                    sp.wait_ge(wk_hi, g + 1)
                    sp.wait_ge(wk_lo, g + 1)
                    sp.wait_ge(wv_hi, g + 1)
                    sp.wait_ge(wv_lo, g + 1)
                    load_qkv(g + 1)
                    sp.wait_ge(wd_hi, 4 * (g + 1))
                    sp.wait_ge(wd_lo, 4 * (g + 1))
                    load_d(g + 1)
                if last and tb == 0:
                    sp.wait_ge(c_hi, BLOCKS)
                    sp.wait_ge(c_lo, BLOCKS)
                    sp.dma_start(ff_raw, qw.rearrange("c p n -> p c n")).then_inc(ff_ld, 16)
                    sp.dma_start(ff_rows[:, ZERO_ROW, :], w_zero.partition_broadcast(P)).then_inc(ff_ld, 16)
                    sp.dma_start(ff_rows[:, SCALE_ROW, :], w_scale.partition_broadcast(P)).then_inc(ff_ld, 16)
                    sp.dma_start(ff_rows[:, BIAS_ROW, :], bias.partition_broadcast(P)).then_inc(ff_ld, 16)
                if last and tb > 1:
                    store(tb - 2)
                if not (last and tb == BLOCKS - 1):
                    duplicate_v(m, tbm % 2)

            def store(tb):
                for t in range(tb * TILES, (tb + 1) * TILES):
                    sp.wait_ge(f_out, t + 1)
                    sp.dma_start(out[t], xacc[:, t, :]).then_inc(stored, 16)

            groups(sp, step)
            store(BLOCKS - 2)
            store(BLOCKS - 1)
            sp.wait_ge(stored, 16 * BLOCKS * TILES)

        @block.gpsimd
        def _(pool):
            pool.memset(ident[:, :], 0.0).then_inc(const_0, 1)
            pool.memset(mask[:, :, :], 0.0).then_inc(const_0, 1)
            pool.wait_ge(const_0, 2)
            pool.affine_select(out=ident[:, :], in_=ident[:, :], compare_op=ALU.not_equal, fill=1.0, base=0,
                               pattern=[[-1, P]], channel_multiplier=1).then_inc(const_ok, 1)
            for half in range(2):
                pool.wait_ge(const_ok, half + 1)
                rows = mask[half * S:(half + 1) * S, 0, :]
                pool.affine_select(out=rows, in_=rows, compare_op=ALU.is_ge, fill=MASKED, base=0,
                                   pattern=[[-1, S]], channel_multiplier=1).then_inc(const_ok, 1)

            def reduce_ctx(tb):
                pool.wait_ge(c_max_ok, tb + 1)
                pool.partition_all_reduce(c_all[:, tb:tb + 1], c_max[:, tb:tb + 1], P,
                                          bass.bass_isa.ReduceOp.max).then_inc(c_red_ok, 1)

            def reduce_w(g):
                pool.wait_ge(w_max_ok, 4 * (g + 1))
                pool.sem_inc(w_max_seen, 1)
                pool.partition_all_reduce(w_all[:, :], w_max[:, :], P,
                                          bass.bass_isa.ReduceOp.max).then_inc(w_red_ok, 1)

            pool.wait_ge(const_ok, 3)
            reduce_w(0)
            pool.wait_ge(w_red_ok, 1)
            reduce_ctx(0)
            pool.wait_ge(c_red_ok, 1)
            reduce_ctx(1)

            def step(g, tb, first, last):
                if first and tb in (1, 2):
                    reduce_ctx(tb + 1)
                if not last and tb == (2 if first else 1):
                    reduce_w(g + 1)
                if last and tb > 0:
                    residual(tb - 1)

            def residual(tb):
                for t in range(tb * TILES, (tb + 1) * TILES):
                    if t == 0:
                        pool.wait_ge(row_ok, 3)
                    pool.wait_ge(xn_ok, BLOCKS * TILES + t + 1)
                    pool.tensor_tensor(xacc[:, t, :], xacc[:, t, :], ff_rows[:, BIAS_ROW, :],
                                       ALU.add).then_inc(xb_ok, 1)

            groups(pool, step)
            residual(BLOCKS - 1)

        @block.scalar
        def _(act):
            def split_ctx(tb):
                act.wait_ge(c_ld[tb], 16)
                act.wait_ge(c_mul_ok, tb + 1)
                act.activation(cT[:, HI, :, toks(tb)], c_raw[:, tb % 2, :].rearrange("p (k n) -> p k n", k=KC),
                               ACT.Copy, scale=c_mul[:, tb:tb + 1]).then_inc(c_hi, 1)

            def split_wq(g, h):
                if h == 0:
                    act.wait_ge(w_mul_ok, g + 1)
                act.activation(wq[:, HI, h, :, :], raw_q[:, h, :, :], ACT.Copy,
                               scale=w_mul[:, 0:1]).then_inc(wq_hi, 1)

            def split_wk(g):
                act.wait_ge(w_mul_ok, g + 1)
                act.activation(wk[:, HI, :, :], raw_k[:, :, :], ACT.Copy, scale=w_mul[:, 1:2]).then_inc(wk_hi, 1)

            def split_wv(g):
                act.activation(wv[:, HI, :, :], raw_v[:, :, :], ACT.Copy, scale=w_mul[:, 2:3]).then_inc(wv_hi, 1)

            def split_wd(g):
                wait(act, y_mm, 16 * g)
                for h in range(HPG):
                    act.activation(wd[:, HI, h, :], raw_d[:, h, :], ACT.Copy, scale=w_mul[:, 3:4]).then_inc(wd_hi, 1)

            def q_part(m, h):
                act.wait_ge(q_mm, 4 * m + h + 1)
                act.activation(q[:, HI, :, h, :], pa[h % 2][:, :].rearrange("p (b s) -> p b s", b=BPB), ACT.Copy,
                               scale=Q_SCALE).then_inc(q_hi, 1)

            def k_part(m):
                act.wait_ge(k_mm, m + 1)
                act.activation(k[:, HI, :], pa[0][:, :], ACT.Copy, scale=K_SCALE).then_inc(k_hi, 1)

            def v_part(m, par):
                act.wait_ge(v_mm, m + 1)
                wait(act, v_dup_ld[1 - par], 32 * (m + par))
                act.activation(v_nat[:, :, HI, :], pa[1][:, :].rearrange("p (t n) -> p t n", t=TILES), ACT.Copy,
                               scale=K_SCALE).then_inc(v_hi, 1)

            def ln_hi(t, summed):
                act.wait_ge(xn_ok, t + 1)
                wait(act, xT_mm, t - 1)
                act.activation(xh[:, t % 2, HI, :], xn[:, t % 2, :], ACT.Copy,
                               accum_out=x_sum[:, t - BLOCKS * TILES:t - BLOCKS * TILES + 1] if summed else None).then_inc(x_hi, 1)

            def ln_out(t):
                act.wait_ge(xT_mm, t + 1)
                at = t % (BLOCKS * TILES) * P
                act.copy(xT[:, :, :, at:at + P],
                         av[t % 2][:, :].bitcast(F16).rearrange("p (c k n) -> p c k n", c=2, k=KC)).then_inc(xT_ok, 1)

            def exp(n, p):
                act.wait_ge(shifted, 2 * n + p + 1)
                act.activation(sc[:, p, :, :], sc[:, p, :, :], ACT.Exp).then_inc(exp_ok, 1)

            def p_part(n, p):
                act.wait_ge(norm_ok, 2 * n + p + 1)
                act.copy(pr[:, p, :, HI, :], sc[:, p, :, :]).then_inc(p_hi, 1)

            def p_transposed(n, p):
                act.wait_ge(pT_mm, 2 * n + p + 1)
                act.copy(pT[:, :, 2 * p:2 * p + 2, :],
                         pp[:, :].bitcast(F16).rearrange("p (b e s) -> p b e s", b=BPB, e=2)).then_inc(pT_ok, 1)

            def av_part(n, j):
                act.wait_ge(av_mm, 4 * n + j + 1)
                for bb in range(2):
                    at = (2 * j + bb) * S
                    last = act.activation(att[:, HI, :, at:at + S],
                                          av[j % 2][:, bb * 256:(bb + 1) * 256].rearrange("p (h s) -> p h s", h=HPG),
                                          ACT.Copy, scale=AV_SCALE)
                last.then_inc(av_hi, 1)

            def block_tiles(tb, base, summed):
                t0 = base + tb * TILES
                ln_hi(t0, summed)
                for t in range(t0 + 1, t0 + TILES):
                    ln_hi(t, summed)
                    ln_out(t - 1)
                ln_out(t0 + TILES - 1)

            def next_weights(g, part):
                if part == 0:
                    for h in range(HPG):
                        split_wq(g, h)
                else:
                    split_wk(g)
                    split_wv(g)

            block_tiles(0, 0, False)
            act.wait_ge(g_ld, 32)
            act.activation(tg[:, :], gates[:, :], ACT.Tanh).then_inc(tanh_ok, 1)
            next_weights(0, 0)
            next_weights(0, 1)
            split_ctx(0)
            q_part(0, 0)
            q_part(0, 1)
            ln_hi(TILES, False)
            q_part(0, 2)
            ln_hi(TILES + 1, False)
            ln_out(TILES)
            q_part(0, 3)
            ln_hi(TILES + 2, False)
            ln_out(TILES + 1)
            k_part(0)
            ln_hi(TILES + 3, False)
            ln_out(TILES + 2)
            v_part(0, 0)
            ln_out(TILES + 3)

            def step(g, tb, first, last):
                n = 4 * g + tb
                gm, tbm, m = following(g, tb)
                ahead = not (last and tb == BLOCKS - 1)
                reweigh = tb == 2 and not last
                ln = (tb + 2) * TILES if first and tb < 2 else (BLOCKS + tb - 1) * TILES if last and tb > 0 else None
                if ahead:
                    q_part(m, 0)
                exp(n, 0)
                if tb == 0:
                    if not first:
                        act.wait_ge(wd_ld, 16 * (g + 1))
                    split_wd(g)
                if ahead:
                    q_part(m, 1)
                p_part(n, 0)
                exp(n, 1)
                if ahead:
                    q_part(m, 2)
                p_part(n, 1)
                if first and tb < 3:
                    split_ctx(tb + 1)
                if ahead:
                    q_part(m, 3)
                p_transposed(n, 0)
                if ahead:
                    k_part(m)
                p_transposed(n, 1)
                av_part(n, 0)
                av_part(n, 1)
                if ahead:
                    v_part(m, tbm % 2)
                av_part(n, 2)
                if reweigh:
                    next_weights(g + 1, 0)
                if ln is not None:
                    ln_hi(ln, last)
                av_part(n, 3)
                if reweigh:
                    next_weights(g + 1, 1)
                if ln is not None:
                    for t in range(ln + 1, ln + TILES):
                        ln_hi(t, last)
                        ln_out(t - 1)
                    ln_out(ln + TILES - 1)

            groups(act, step)
            block_tiles(BLOCKS - 1, BLOCKS * TILES, True)

        @block.vector
        def _(dve):
            def power_of_two(raw, guarded, pow2, inverse, factor, cols, red_ok, grd_ok, pow_ok, inv_ok_, mul_ok, count):
                dve.wait_ge(red_ok, count)
                dve.tensor_scalar(guarded[:, cols], raw[:, cols], 1e-30, None, ALU.max).then_inc(grd_ok, 1)
                dve.wait_ge(grd_ok, count)
                dve.tensor_scalar(pow2[:, cols].bitcast(I32), guarded[:, cols].bitcast(I32), EXPONENT, None,
                                  ALU.bitwise_and).then_inc(pow_ok, 1)
                dve.wait_ge(pow_ok, count)
                dve.reciprocal(inverse[:, cols], pow2[:, cols]).then_inc(inv_ok_, 1)
                dve.wait_ge(inv_ok_, count)
                dve.tensor_scalar(factor[:, cols], inverse[:, cols], W_SCALE, None, ALU.mult).then_inc(mul_ok, 1)

            def ctx_max(tb):
                dve.wait_ge(c_ld[tb], 16)
                dve.tensor_reduce(c_max[:, tb:tb + 1], c_raw[:, tb % 2, :], AX.X, ALU.max,
                                  apply_absolute_value=True).then_inc(c_max_ok, 1)

            def ctx_lo(tb):
                power_of_two(c_all, c_grd, c_pow, c_inv, c_mul, slice(tb, tb + 1),
                             c_red_ok, c_grd_ok, c_pow_ok, c_inv_ok, c_mul_ok, tb + 1)
                dve.wait_ge(c_mul_ok, tb + 1)
                dve.wait_ge(c_hi, tb + 1)
                for kc in range(KC):
                    last = dve.scalar_tensor_tensor(out=cT[:, LO, kc, toks(tb)],
                                                    in0=c_raw[:, tb % 2, kc * BT:(kc + 1) * BT],
                                                    scalar=c_mul[:, tb:tb + 1], in1=cT[:, HI, kc, toks(tb)],
                                                    op0=ALU.mult, op1=ALU.subtract)
                last.then_inc(c_lo, 1)

            def weight_max(g, which):
                if 0 in which:
                    dve.wait_ge(wqkv_ld, 48 * (g + 1))
                for i, raw in enumerate((raw_q[:, :, :, :].rearrange("p h k n -> p (h k n)"),
                                         raw_k[:, :, :].rearrange("p k n -> p (k n)"),
                                         raw_v[:, :, :].rearrange("p k n -> p (k n)"),
                                         raw_d[:, :, :].rearrange("p h n -> p (h n)"))):
                    if i not in which:
                        continue
                    if i == 3:
                        dve.wait_ge(wd_ld, 16 * (g + 1))
                    dve.tensor_reduce(w_max[:, i:i + 1], raw, AX.X, ALU.max,
                                      apply_absolute_value=True).then_inc(w_max_ok, 1)

            def weight_scale(g):
                power_of_two(w_all, w_grd, w_pow, w_inv, w_mul, slice(0, 4),
                             w_red_ok, w_grd_ok, w_pow_ok, w_inv_ok, w_mul_ok, g + 1)
                for i in range(2):
                    dve.tensor_tensor(w_prod[:, i:i + 1], w_pow[:, 2 * i:2 * i + 1], w_pow[:, 2 * i + 1:2 * i + 2],
                                      ALU.mult).then_inc(w_prod_ok, 1)
                dve.wait_ge(w_mul_ok, g + 1)

            def unscale(g, cols, count):
                if cols.start == 0:
                    dve.wait_ge(w_prod_ok, 2 * (g + 1))
                    dve.tensor_copy(w_now[:, :], w_prod[:, :]).then_inc(w_now_ok, 1)
                    dve.wait_ge(w_now_ok, g + 1)
                dve.tensor_scalar(f_score[:, cols], c_pow[:, cols], w_now[:, 0:1], SCORE_UNSCALE,
                                  ALU.mult, ALU.mult).then_inc(f_ok, 1)
                wait(dve, y_ok, 16 * g)
                dve.tensor_scalar(f_y[:, cols], c_pow[:, cols], w_now[:, 1:2], tgy[:, 0:1],
                                  ALU.mult, ALU.mult).then_inc(f_ok, 1)
                dve.wait_ge(f_ok, count)

            def lo_part(out, in0, scale, hi, done):
                dve.scalar_tensor_tensor(out=out, in0=in0, scalar=scale, in1=hi,
                                         op0=ALU.mult, op1=ALU.subtract).then_inc(done, 1)

            def split_wq(g, h):
                dve.wait_ge(wq_hi, 4 * g + h + 1)
                lo_part(wq[:, LO, h, :, :], raw_q[:, h, :, :], w_mul[:, 0:1], wq[:, HI, h, :, :], wq_lo)

            def split_wk(g):
                dve.wait_ge(wk_hi, g + 1)
                lo_part(wk[:, LO, :, :], raw_k[:, :, :], w_mul[:, 1:2], wk[:, HI, :, :], wk_lo)

            def split_wv(g):
                dve.wait_ge(wv_hi, g + 1)
                lo_part(wv[:, LO, :, :], raw_v[:, :, :], w_mul[:, 2:3], wv[:, HI, :, :], wv_lo)

            def split_wd(g):
                for h in range(HPG):
                    dve.wait_ge(wd_hi, 4 * g + h + 1)
                    lo_part(wd[:, LO, h, :], raw_d[:, h, :], w_mul[:, 3:4], wd[:, HI, h, :], wd_lo)

            def q_part(m, h):
                dve.wait_ge(q_hi, 4 * m + h + 1)
                lo_part(q[:, LO, :, h, :], pa[h % 2][:, :].rearrange("p (b s) -> p b s", b=BPB), Q_SCALE,
                        q[:, HI, :, h, :], q_lo)

            def k_part(m):
                dve.wait_ge(k_hi, m + 1)
                lo_part(k[:, LO, :], pa[0][:, :], K_SCALE, k[:, HI, :], k_lo)

            def v_part(m):
                dve.wait_ge(v_hi, m + 1)
                lo_part(v_nat[:, :, LO, :], pa[1][:, :].rearrange("p (t n) -> p t n", t=TILES), K_SCALE,
                        v_nat[:, :, HI, :], v_lo)

            def scores(n, tb, p):
                dve.wait_ge(s_mm, 2 * n + p + 1)
                dve.scalar_tensor_tensor(out=sc[:, p, :, :], in0=ps[:, :].rearrange("p (b s) -> p b s", b=BPB),
                                         scalar=f_score[:, tb:tb + 1], in1=mask[:, :, :].to_broadcast([P, BPB, S]),
                                         op0=ALU.mult, op1=ALU.add).then_inc(s_masked, 1)
                dve.wait_ge(s_masked, 2 * n + p + 1)
                dve.tensor_reduce(row_max[:, p, :], sc[:, p, :, :], AX.X, ALU.max).then_inc(max_ok, 1)
                dve.wait_ge(max_ok, 2 * n + p + 1)
                dve.tensor_tensor(sc[:, p, :, :], sc[:, p, :, :],
                                  row_max[:, p, :].unsqueeze(2).to_broadcast([P, BPB, S]),
                                  ALU.subtract).then_inc(shifted, 1)

            def normalise(n, p):
                dve.wait_ge(exp_ok, 2 * n + p + 1)
                dve.tensor_reduce(row_sum[:, p, :], sc[:, p, :, :], AX.X, ALU.add).then_inc(sum_ok, 1)
                dve.wait_ge(sum_ok, 2 * n + p + 1)
                dve.reciprocal(row_inv[:, p, :], row_sum[:, p, :]).then_inc(inv_ok, 1)
                dve.wait_ge(inv_ok, 2 * n + p + 1)
                dve.scalar_tensor_tensor(out=sc[:, p, :, :], in0=sc[:, p, :, :], scalar=P_SCALE,
                                         in1=row_inv[:, p, :].unsqueeze(2).to_broadcast([P, BPB, S]),
                                         op0=ALU.mult, op1=ALU.mult).then_inc(norm_ok, 1)

            def p_part(n, p):
                dve.wait_ge(p_hi, 2 * n + p + 1)
                dve.tensor_tensor(pr[:, p, :, LO, :], sc[:, p, :, :], pr[:, p, :, HI, :],
                                  ALU.subtract).then_inc(p_lo, 1)

            def av_part(n, j):
                dve.wait_ge(av_hi, 4 * n + j + 1)
                for bb in range(2):
                    at = (2 * j + bb) * S
                    last = dve.scalar_tensor_tensor(
                        out=att[:, LO, :, at:at + S],
                        in0=av[j % 2][:, bb * 256:(bb + 1) * 256].rearrange("p (h s) -> p h s", h=HPG),
                        scalar=AV_SCALE, in1=att[:, HI, :, at:at + S], op0=ALU.mult, op1=ALU.subtract)
                last.then_inc(av_lo, 1)

            def y_part(n, tb, j):
                dve.wait_ge(y_mm, 4 * n + j + 1)
                t = tb * TILES + j
                dve.scalar_tensor_tensor(out=xacc[:, t, :], in0=py[j % 2][:, :], scalar=f_y[:, tb:tb + 1],
                                         in1=xacc[:, t, :], op0=ALU.mult, op1=ALU.add).then_inc(y_ok, 1)

            def ln_stats(tb, second):
                call = tb + (BLOCKS if second else 0)
                if second:
                    dve.wait_ge(y_ok, 4 * (BLOCKS * (GROUPS - 1) + tb + 1))
                else:
                    dve.wait_ge(x_ld[tb], 16)
                for t in range(TILES):
                    dve.bn_stats(bn[:, t, :], xacc[:, tb * TILES + t, :]).then_inc(bn_ok, 1)
                for t in range(TILES):
                    dve.wait_ge(bn_ok, TILES * call + t + 1)
                    dve.bn_aggr(mv[:, t, :], bn[:, t, :]).then_inc(mv_ok, 1)
                dve.wait_ge(mv_ok, TILES * (call + 1))
                count = 13 * call

                def chained(ins):
                    nonlocal count
                    count += 1
                    ins.then_inc(rs_ok, 1)
                    dve.wait_ge(rs_ok, count)

                chained(dve.tensor_scalar(var_e[:, :], mv[:, :, 1], LN_EPS, None, ALU.add))
                chained(dve.tensor_scalar(rs[:, 4, :].bitcast(I32), var_e[:, :].bitcast(I32), 1, None,
                                          ALU.logical_shift_right))
                chained(dve.tensor_scalar(rs[:, 0, :].bitcast(I32), rs[:, 4, :].bitcast(I32), -1.0, float(RSQRT_MAGIC),
                                          ALU.mult, ALU.add))
                for i in range(3):
                    y = rs[:, i, :]
                    chained(dve.tensor_tensor(rs_t[:, 0, :], y, y, ALU.mult))
                    chained(dve.scalar_tensor_tensor(out=rs_t[:, 1, :], in0=rs_t[:, 0, :], scalar=-0.5, in1=var_e[:, :],
                                                     op0=ALU.mult, op1=ALU.mult))
                    chained(dve.scalar_tensor_tensor(out=rs[:, i + 1, :], in0=rs_t[:, 1, :], scalar=1.5, in1=y,
                                                     op0=ALU.add, op1=ALU.mult))
                chained(dve.tensor_scalar(rstd[:, :], rs[:, 3, :], XN_SCALE, None, ALU.mult))

            def ln_tile(t):
                wait(dve, x_hi, t - 1)
                at = t % TILES
                dve.tensor_scalar(xn[:, t % 2, :], xacc[:, t % (BLOCKS * TILES), :], mv[:, at, 0:1], rstd[:, at:at + 1],
                                  ALU.subtract, ALU.mult).then_inc(xn_ok, 1)
                dve.wait_ge(xn_ok, t + 1)
                dve.wait_ge(x_hi, t + 1)
                dve.tensor_tensor(xh[:, t % 2, LO, :], xn[:, t % 2, :], xh[:, t % 2, HI, :],
                                  ALU.subtract).then_inc(x_lo, 1)

            def ffn_weights():
                dve.wait_ge(ff_ld, 64)
                for j, (word, shift) in enumerate(((0, 0), (0, 6), (1, 0), (2, 0))):
                    dve.tensor_scalar(xn[:, j % 2, :].bitcast(I32), ff_raw[:, word, :], shift, 63,
                                      ALU.logical_shift_right, ALU.bitwise_and).then_inc(ffw_int, 1)
                    dve.wait_ge(ffw_int, j + 1)
                    dve.tensor_copy(ff_w[:, j, :], xn[:, j % 2, :].bitcast(I32)).then_inc(ffw_ok, 1)
                dve.tensor_scalar(ff_rows[:, ZERO_ROW, :], ff_rows[:, ZERO_ROW, :], -1.0, None,
                                  ALU.mult).then_inc(row_ok, 1)
                dve.tensor_scalar(ff_rows[:, SCALE_ROW, :], ff_rows[:, SCALE_ROW, :], tg[:, 1:2], 1.0 / XN_SCALE,
                                  ALU.mult, ALU.mult).then_inc(row_ok, 1)
                dve.tensor_scalar(ff_rows[:, BIAS_ROW, :], ff_rows[:, BIAS_ROW, :], tg[:, 1:2], None,
                                  ALU.mult).then_inc(row_ok, 1)

            def ffn_out(t):
                dve.wait_ge(f_mm, t + 1)
                dve.scalar_tensor_tensor(out=xs[:, t % 2, :], in0=ff_rows[:, ZERO_ROW, :],
                                         scalar=x_sum[:, t:t + 1],
                                         in1=py[t % 2][:, :], op0=ALU.mult, op1=ALU.add).then_inc(f_zero, 1)
                dve.wait_ge(f_zero, t + 1)
                dve.tensor_tensor(xs[:, t % 2, :], xs[:, t % 2, :], ff_rows[:, SCALE_ROW, :],
                                  ALU.mult).then_inc(f_scaled, 1)
                dve.wait_ge(f_scaled, t + 1)
                dve.wait_ge(xb_ok, t + 1)
                dve.tensor_tensor(xacc[:, t, :], xacc[:, t, :], xs[:, t % 2, :], ALU.add).then_inc(f_out, 1)

            ln_stats(0, False)
            for t in range(TILES):
                ln_tile(t)
            weight_max(0, range(4))
            ctx_max(0)
            weight_scale(0)
            for h in range(HPG):
                split_wq(0, h)
            split_wk(0)
            split_wv(0)
            ctx_lo(0)
            dve.wait_ge(tanh_ok, 1)
            dve.tensor_scalar(tgy[:, :], tg[:, 0:1], Y_UNSCALE, None, ALU.mult).then_inc(tgy_ok, 1)
            dve.wait_ge(tgy_ok, 1)
            q_part(0, 0)
            ln_stats(1, False)
            for h in range(1, HPG):
                q_part(0, h)
                ln_tile(TILES + h - 1)
            k_part(0)
            ln_tile(2 * TILES - 1)
            v_part(0)
            ctx_max(1)

            def step(g, tb, first, last):
                n = 4 * g + tb
                gm, tbm, m = following(g, tb)
                ahead = not (last and tb == BLOCKS - 1)
                reweigh = tb == 2 and not last
                ln = (tb + 2) * TILES if first and tb < 2 else (BLOCKS + tb - 1) * TILES if last and tb > 0 else None
                if first:
                    if tb == 0:
                        dve.wait_ge(const_ok, 3)
                    unscale(g, slice(tb, tb + 1), 2 * (tb + 1))
                elif tb == 0:
                    unscale(g, slice(0, BLOCKS), 2 * BLOCKS + 2 * g)
                scores(n, tb, 0)
                if ahead:
                    q_part(m, 0)
                scores(n, tb, 1)
                normalise(n, 0)
                if ahead:
                    q_part(m, 1)
                p_part(n, 0)
                if first and tb in (1, 2):
                    ctx_max(tb + 1)
                normalise(n, 1)
                if ahead:
                    q_part(m, 2)
                p_part(n, 1)
                if first and tb < 3:
                    ctx_lo(tb + 1)
                if reweigh and not first:
                    weight_scale(g + 1)
                if last and tb > 1:
                    for t in range(TILES):
                        ffn_out((tb - 2) * TILES + t)
                if ahead:
                    q_part(m, 3)
                if tb == 0:
                    split_wd(g)
                if ahead:
                    k_part(m)
                if reweigh and first:
                    weight_max(g + 1, range(4))
                if ln is not None:
                    ln_stats(ln // TILES % BLOCKS, last)
                av_part(n, 0)
                av_part(n, 1)
                if ahead:
                    v_part(m)
                if reweigh and first:
                    weight_scale(g + 1)
                for j in range(TILES):
                    if ln is not None:
                        ln_tile(ln + j)
                    y_part(n, tb, j)
                    if j < 2:
                        av_part(n, j + 2)
                    if tb == 1 and not first and not last:
                        weight_max(g + 1, ((0,), (1, 2), (3,), ())[j])
                    if reweigh:
                        if j < 2:
                            split_wq(g + 1, 2 * j)
                            split_wq(g + 1, 2 * j + 1)
                        elif j == 2:
                            split_wk(g + 1)
                            split_wv(g + 1)
                if last and tb == 0:
                    ffn_weights()

            groups(dve, step)
            ln_stats(BLOCKS - 1, True)
            for t in range((BLOCKS - 1) * TILES, BLOCKS * TILES):
                ln_tile(BLOCKS * TILES + t)
                ffn_out(t - TILES)
            for t in range((BLOCKS - 1) * TILES, BLOCKS * TILES):
                ffn_out(t)

        @block.tensor
        def _(pe):
            def product(out, stationary, moving, count):
                for i in range(count):
                    for a, b in PASSES:
                        last = pe.matmul(out, stationary(a, i), moving(b, i),
                                         start=(i == 0 and (a, b) == PASSES[0]),
                                         stop=(i == count - 1 and (a, b) == PASSES[-1]))
                return last

            def q_unit(gm, tbm, m, h, in_first):
                pe.wait_ge(wq_hi, 4 * gm + h + 1)
                pe.wait_ge(wq_lo, 4 * gm + h + 1)
                if h == 0:
                    if in_first:
                        pe.wait_ge(xT_ok, TILES * (tbm + 1))
                    wait(pe, k_hi, m)
                    wait(pe, k_lo, m)
                elif h == 1:
                    wait(pe, v_hi, m)
                    wait(pe, v_lo, m)
                else:
                    pe.wait_ge(q_hi, 4 * m + h - 1)
                    pe.wait_ge(q_lo, 4 * m + h - 1)
                product(pa[h % 2][:, :], lambda a, i: wq[:, a, h, i, :], lambda b, i: xT[:, b, i, toks(tbm)],
                        KC).then_inc(q_mm, 1)

            def k_unit(gm, tbm, m, in_first):
                pe.wait_ge(wk_hi, gm + 1)
                pe.wait_ge(wk_lo, gm + 1)
                if in_first:
                    pe.wait_ge(c_hi, tbm + 1)
                    pe.wait_ge(c_lo, tbm + 1)
                pe.wait_ge(q_hi, 4 * m + 3)
                pe.wait_ge(q_lo, 4 * m + 3)
                product(pa[0][:, :], lambda a, i: wk[:, a, i, :], lambda b, i: cT[:, b, i, toks(tbm)],
                        KC).then_inc(k_mm, 1)

            def v_unit(gm, tbm, m, tiles):
                if 0 in tiles:
                    pe.wait_ge(wv_hi, gm + 1)
                    pe.wait_ge(wv_lo, gm + 1)
                    pe.wait_ge(q_hi, 4 * m + 4)
                    pe.wait_ge(q_lo, 4 * m + 4)
                for t in tiles:
                    at = tbm * BT + t * P
                    last = product(pa[1][:, t * P:(t + 1) * P], lambda a, i: cT[:, a, i, at:at + P],
                                   lambda b, i: wv[:, b, i, :], KC)
                if TILES - 1 in tiles:
                    last.then_inc(v_mm, 1)

            def score_unit(n, p):
                pe.wait_ge(q_hi, 4 * n + 2 * p + 2)
                pe.wait_ge(q_lo, 4 * n + 2 * p + 2)
                if p == 0:
                    pe.wait_ge(k_hi, n + 1)
                    pe.wait_ge(k_lo, n + 1)
                wait(pe, s_masked, 2 * n + p)
                for b in range(BPB):
                    for a, c in PASSES:
                        last = pe.matmul(ps[:, b * S:(b + 1) * S],
                                         q[:, a, b, 2 * p:2 * p + 2, :].rearrange("p e s -> p (e s)"),
                                         k[:, c, b * S:(b + 1) * S],
                                         start=((a, c) == PASSES[0]), stop=((a, c) == PASSES[-1]))
                last.then_inc(s_mm, 1)

            def p_transpose(n, p):
                pe.wait_ge(p_hi, 2 * n + p + 1)
                pe.wait_ge(p_lo, 2 * n + p + 1)
                wait(pe, pT_ok, 2 * n + p)
                bank16 = pp[:, :].bitcast(F16)
                for b in range(BPB):
                    last = pe.transpose(bank16[:, b * P:(b + 1) * P],
                                        pr[:, p, b, :, :].rearrange("p c s -> p (c s)"), ident[:, :])
                last.then_inc(pT_mm, 1)

            def av_unit(n, par, j):
                if j == 0:
                    pe.wait_ge(pT_ok, 2 * n + 2)
                    pe.wait_ge(v_dup_ld[par], 32 * (n + 2 - par))
                wait(pe, av_hi, 4 * n + j - 1)
                wait(pe, av_lo, 4 * n + j - 1)
                for bb in range(2):
                    b = 2 * j + bb
                    for c in (HI, LO):
                        last = pe.matmul(av[j % 2][:, bb * 256:(bb + 1) * 256], v_dup[:, par, b, c, :],
                                         pT[:, b, :, :].rearrange("p h s -> p (h s)"),
                                         start=(c == HI), stop=(c == LO))
                last.then_inc(av_mm, 1)

            def y_unit(g, n, j):
                if j == 0:
                    pe.wait_ge(wd_hi, 4 * (g + 1))
                    pe.wait_ge(wd_lo, 4 * (g + 1))
                pe.wait_ge(av_hi, 4 * n + j + 1)
                pe.wait_ge(av_lo, 4 * n + j + 1)
                wait(pe, y_ok, 4 * n + j - 1)
                product(py[j % 2][:, :], lambda a, h: att[:, a, h, j * P:(j + 1) * P],
                        lambda b, h: wd[:, b, h, :], HPG).then_inc(y_mm, 1)

            def ln_transpose(t, av_before):
                pe.wait_ge(x_hi, t + 1)
                pe.wait_ge(x_lo, t + 1)
                wait(pe, xT_ok, t - 1)
                wait(pe, av_hi, av_before)
                wait(pe, av_lo, av_before)
                bank16 = av[t % 2][:, :].bitcast(F16)
                for c in (HI, LO):
                    for i in range(KC):
                        if t < BLOCKS * TILES:
                            part = xh[:, t % 2, c, i * P:(i + 1) * P]
                        else:
                            part = xh[:, t % 2, c, :].rearrange("p (i j) -> p j i", j=KC)[:, i, :]
                        at = (c * KC + i) * P
                        last = pe.transpose(bank16[:, at:at + P], part, ident[:, :])
                last.then_inc(xT_mm, 1)

            def ffn_unit(t, y_before):
                if t == 0:
                    pe.wait_ge(ffw_ok, 4)
                pe.wait_ge(xT_ok, BLOCKS * TILES + t + 1)
                if t % TILES < 2:
                    pe.wait_ge(y_ok, y_before)
                wait(pe, f_zero, t - 1)
                for i in range(KC):
                    for a in (HI, LO):
                        last = pe.matmul(py[t % 2][:, :], xT[:, a, i, t * P:(t + 1) * P], ff_w[:, i, :],
                                         start=(i == 0 and a == HI), stop=(i == KC - 1 and a == LO))
                last.then_inc(f_mm, 1)

            pe.wait_ge(const_ok, 1)
            for t in range(TILES):
                ln_transpose(t, 0)
            for h in range(HPG):
                q_unit(0, 0, 0, h, True)
                if h >= 2:
                    ln_transpose(TILES + h - 2, 0)
            k_unit(0, 0, 0, True)
            ln_transpose(TILES + 2, 0)
            v_unit(0, 0, 0, range(TILES))
            ln_transpose(TILES + 3, 0)

            def step(g, tb, first, last):
                n = 4 * g + tb
                gm, tbm, m = following(g, tb)
                ahead = not (last and tb == BLOCKS - 1)
                in_first = first and tbm > 0
                ln = (tb + 2) * TILES if first and tb < 2 else (BLOCKS + tb - 1) * TILES if last and tb > 0 else None
                ffn = last and tb > 1
                score_unit(n, 0)
                if ahead:
                    q_unit(gm, tbm, m, 0, in_first)
                score_unit(n, 1)
                if ahead:
                    q_unit(gm, tbm, m, 1, in_first)
                    q_unit(gm, tbm, m, 2, in_first)
                if ffn:
                    for t in range(TILES):
                        ffn_unit((tb - 2) * TILES + t, 4 * n)
                if ahead:
                    q_unit(gm, tbm, m, 3, in_first)
                p_transpose(n, 0)
                if ahead:
                    k_unit(gm, tbm, m, in_first)
                p_transpose(n, 1)
                if ahead:
                    v_unit(gm, tbm, m, range(TILES // 2))
                if first and tb < 3:
                    pe.wait_ge(xT_ok, (tb + 2) * TILES if tb < 2 else BLOCKS * TILES)
                elif last and tb > 1:
                    pe.wait_ge(xT_ok, (BLOCKS + tb - 1) * TILES)
                av_unit(n, tb % 2, 0)
                av_unit(n, tb % 2, 1)
                if ahead:
                    v_unit(gm, tbm, m, range(TILES // 2, TILES))
                if ffn:
                    pe.wait_ge(f_zero, (tb - 1) * TILES)
                y_unit(g, n, 0)
                av_unit(n, tb % 2, 2)
                y_unit(g, n, 1)
                av_unit(n, tb % 2, 3)
                if ln is not None:
                    ln_transpose(ln, 4 * n + 4)
                y_unit(g, n, 2)
                if ln is not None:
                    ln_transpose(ln + 1, 4 * n + 4)
                y_unit(g, n, 3)
                if ln is not None:
                    ln_transpose(ln + 2, 4 * n + 4)
                    ln_transpose(ln + 3, 4 * n + 4)

            groups(pe, step)
            ffn_unit((BLOCKS - 2) * TILES, 4 * BLOCKS * GROUPS)
            for t in range((BLOCKS - 1) * TILES, BLOCKS * TILES):
                ffn_unit(t - TILES + 1, 4 * BLOCKS * GROUPS)
                ln_transpose(BLOCKS * TILES + t, 4 * BLOCKS * GROUPS)
            for t in range((BLOCKS - 1) * TILES + 1, BLOCKS * TILES):
                ffn_unit(t, 4 * BLOCKS * GROUPS)


def kernel(**inputs):
    import numpy as np
    import concourse.bacc as bacc
    from concourse.bass_utils import run_bass_kernel_spmd

    a = {name: np.asarray(v) for name, v in inputs.items()}
    laid = {
        "x": a["x"].reshape(BLOCKS * TILES, P, D),
        "ctxT": a["ctx_4096"].reshape(BLOCKS, BT, KC, P).transpose(0, 3, 2, 1).reshape(BLOCKS, P, KC * BT),
        "wqT": a["L0_xattn_Wq"].reshape(GROUPS, HPG, DK, KC, P).transpose(0, 4, 1, 3, 2).reshape(GROUPS, P, HPG * KC * DK),
        "wkT": a["L0_xattn_Wk"].reshape(GROUPS, DK, KC, P).transpose(0, 3, 2, 1).reshape(GROUPS, P, KC * DK),
        "wvT": a["L0_xattn_Wv"].reshape(GROUPS, DK, KC, P).transpose(0, 3, 2, 1).reshape(GROUPS, P, KC * DK),
        "wdT": a["L0_xattn_Wd"].reshape(D, GROUPS, HPG, DK).transpose(1, 3, 2, 0).reshape(GROUPS, DK, HPG * D),
        "g_x": a["g_xattn"].reshape(1),
        "g_f": a["g_ffn"].reshape(1),
        "qw": a["L0_ffn_qweight"].reshape(D, P, 3).transpose(2, 1, 0),
        "w_scale": a["L0_ffn_weight_scale"].reshape(D),
        "w_zero": a["L0_ffn_weight_zero_point"].reshape(D),
        "bias": a["L0_ffn_bias"].reshape(D),
    }
    laid = {name: np.ascontiguousarray(v) for name, v in laid.items()}
    nc = bacc.Bacc("TRN2", target_bir_lowering=False, num_devices=1)
    args = [nc.dram_tensor(f"in_{name}", v.shape, mybir.dt.from_np(v.dtype), kind="ExternalInput").ap()
            for name, v in laid.items()]
    result = nc.dram_tensor("out_x", (BLOCKS * TILES, P, D), F32, kind="ExternalOutput").ap()
    build(nc, *args, result)
    r = run_bass_kernel_spmd(nc, [{f"in_{name}": v for name, v in laid.items()}], core_ids=[0])
    return r.results[0]["out_x"].reshape(B, S, D)
```

```python
from contextlib import ExitStack

import concourse.bass as bass
from concourse import mybir

F32 = mybir.dt.float32
F16 = mybir.dt.float16
I32 = mybir.dt.int32
ALU = mybir.AluOpType
ACT = mybir.ActivationFunctionType
AX = mybir.AxisListType

P = 128
B, S, D = 32, 64, 512
HEADS, GROUPS, DK = 32, 8, 128
HPG = HEADS // GROUPS
KC = D // P
TOKENS = B * S
BT = 512
BLOCKS = TOKENS // BT
TILES = BT // P
BPB = BT // S
PAIRS = HPG // 2
HI, LO = 0, 1
PASSES = ((HI, HI), (HI, LO), (LO, HI))
SLOTS = 3

FFN_POOL_TILES = BLOCKS * TILES - 3
WARM_UP = 16
LN_EPS = 1e-5
XN_SCALE = 2.0 ** 8
W_SCALE = 2.0 ** 12
Q_SCALE = 2.0 ** -15
K_SCALE = 2.0 ** -20
P_SCALE = 2.0 ** 10
AV_SCALE = 2.0 ** -10
SCORE_UNSCALE = 1.0 / (XN_SCALE * W_SCALE * Q_SCALE * W_SCALE * W_SCALE * K_SCALE) * DK ** -0.5
Y_UNSCALE = 1.0 / (W_SCALE * W_SCALE * K_SCALE * W_SCALE)
MASKED = -3.0e38
EXPONENT = 0x7F800000
RSQRT_MAGIC = 0x5F3759DF


def build(nc, x, ctxT, wqT, wkT, wvT, wdT, g_x, g_f, qw, w_scale, w_zero, bias, out):
    with ExitStack() as stack:
        def sb(name, shape, dt=F32):
            return stack.enter_context(nc.sbuf_tensor(name, shape, dt))

        def bank(name):
            return stack.enter_context(nc.psum_tensor(name, [P, BT], F32))

        def sem(name):
            return stack.enter_context(nc.semaphore(name))

        xacc = sb("xacc", [P, BLOCKS * TILES, D])
        xT = sb("xT", [P, 2, KC, TOKENS], F16)
        cT = sb("cT", [P, 2, KC, TOKENS], F16)
        raw_q = sb("raw_q", [P, HPG, KC, DK])
        raw_k = sb("raw_k", [P, KC, DK])
        raw_v = sb("raw_v", [P, KC, DK])
        raw_d = sb("raw_d", [P, HPG, D])
        wq = sb("wq", [P, 2, HPG, KC, DK], F16)
        wk = sb("wk", [P, 2, KC, DK], F16)
        wv = sb("wv", [P, 2, KC, DK], F16)
        wd = sb("wd", [P, 2, HPG, D], F16)
        q = sb("q", [P, 2, BPB, HPG, S], F16)
        k = sb("k", [P, 2, BT], F16)
        v_nat = sb("v_nat", [P, TILES, 2, DK], F16)
        v_dup = sb("v_dup", [P, 2, BPB, 2, DK], F16)
        sc = sb("sc", [P, PAIRS, BPB, S])
        pr = sb("pr", [P, PAIRS, BPB, 2, S], F16)
        pT = sb("pT", [P, BPB, HPG, S], F16)
        att = sb("att", [P, 2, HPG, BT], F16)
        shared = sb("shared", [P, 4096])
        c_raw = shared[:, :].rearrange("p (s n) -> p s n", s=2)
        ff_raw = shared[:, 0:1536].bitcast(I32).rearrange("p (c n) -> p c n", c=3)
        ff_w = shared[:, 1536:2560].bitcast(F16).rearrange("p (j n) -> p j n", j=4)
        ff_rows = shared[:, 2560:4096].rearrange("p (r n) -> p r n", r=3)
        ZERO_ROW, SCALE_ROW, BIAS_ROW = range(3)
        xn = sb("xn", [P, SLOTS, D])
        xh = sb("xh", [P, SLOTS, 2, D], F16)
        xs = ([raw_q[:, i, :, :].rearrange("p k n -> p (k n)") for i in range(HPG)]
              + [raw_d[:, i, :] for i in range(HPG)])
        ident = sb("ident", [P, P], F16)
        mask = sb("mask", [P, 1, S])
        row_max = sb("row_max", [P, PAIRS, BPB])
        row_sum = sb("row_sum", [P, PAIRS, BPB])
        row_inv = sb("row_inv", [P, PAIRS, BPB])
        gates = sb("gates", [P, 2])
        tg = sb("tg", [P, 2])
        tgy = sb("tgy", [P, 1])
        head_max = sb("head_max", [P, HPG])
        w_max = sb("w_max", [P, 4])
        w_all = sb("w_all", [P, 4])
        w_grd = sb("w_grd", [P, 4])
        w_pow = sb("w_pow", [P, 4])
        w_inv = sb("w_inv", [P, 4])
        w_mul = sb("w_mul", [P, 4])
        w_prod = sb("w_prod", [P, 2])
        w_now = sb("w_now", [P, 2])
        f_score = sb("f_score", [P, BLOCKS])
        f_y = sb("f_y", [P, BLOCKS])
        c_max = sb("c_max", [P, BLOCKS])
        c_all = sb("c_all", [P, BLOCKS])
        c_grd = sb("c_grd", [P, BLOCKS])
        c_pow = sb("c_pow", [P, BLOCKS])
        c_inv = sb("c_inv", [P, BLOCKS])
        c_mul = sb("c_mul", [P, BLOCKS])
        bn = sb("bn", [P, TILES, 6])
        mv = sb("mv", [P, TILES, 2])
        var_e = sb("var_e", [P, TILES])
        half_var = sb("half_var", [P, TILES])
        rs_bits = sb("rs_bits", [P, TILES], I32)
        rs = sb("rs", [P, 3, TILES])
        rs_t = sb("rs_t", [P, TILES])
        rstd = sb("rstd", [P, TILES])
        x_sum = sb("x_sum", [P, BLOCKS * TILES])

        pa = [bank("pa0"), bank("pa1")]
        py = [bank("py0"), bank("py1")]
        av = [bank("av0"), bank("av1")]
        ps = bank("ps")
        pp = bank("pp")

        x0_ld = [sem(f"x0_ld{i}") for i in range(TILES)]
        x_ld = [sem(f"x_ld{i}") for i in range(BLOCKS)]
        c_ld = [sem(f"c_ld{i}") for i in range(BLOCKS)]
        g_ld = sem("g_ld")
        wq0_ld = [sem(f"wq0_ld{i}") for i in range(HPG)]
        wq_ld = sem("wq_ld")
        wkv_ld = sem("wkv_ld")
        wd_ld = sem("wd_ld")
        ff_ld = sem("ff_ld")
        v_dup_ld = [sem("v_dup_ld0"), sem("v_dup_ld1")]
        stored = sem("stored")
        const_0 = sem("const_0")
        const_ok = sem("const_ok")
        tanh_ok = sem("tanh_ok")
        tgy_ok = sem("tgy_ok")
        head_max_ok = sem("head_max_ok")
        w_max_ok = sem("w_max_ok")
        w_max_seen = sem("w_max_seen")
        w_red_ok = sem("w_red_ok")
        w_grd_ok = sem("w_grd_ok")
        w_pow_ok = sem("w_pow_ok")
        w_inv_ok = sem("w_inv_ok")
        w_mul_ok = sem("w_mul_ok")
        w_prod_ok = sem("w_prod_ok")
        w_now_ok = sem("w_now_ok")
        f_ok = sem("f_ok")
        wq_hi, wq_lo = sem("wq_hi"), sem("wq_lo")
        wk_hi, wk_lo = sem("wk_hi"), sem("wk_lo")
        wv_hi, wv_lo = sem("wv_hi"), sem("wv_lo")
        wd_hi, wd_lo = sem("wd_hi"), sem("wd_lo")
        c_max_ok, c_red_ok, c_grd_ok, c_pow_ok, c_inv_ok, c_mul_ok = [
            sem(s) for s in ("c_max_ok", "c_red_ok", "c_grd_ok", "c_pow_ok", "c_inv_ok", "c_mul_ok")]
        c_hi, c_scaled, c_lo = sem("c_hi"), sem("c_scaled"), sem("c_lo")
        bn_ok = sem("bn_ok")
        mv_ok = sem("mv_ok")
        seed_ok = sem("seed_ok")
        rs_ok = sem("rs_ok")
        xn_ok = sem("xn_ok")
        x_hi, x_lo = sem("x_hi"), sem("x_lo")
        xT_mm = sem("xT_mm")
        xT_ok = sem("xT_ok")
        q_mm, q_hi, q_lo = sem("q_mm"), sem("q_hi"), sem("q_lo")
        k_mm, k_hi, k_lo = sem("k_mm"), sem("k_hi"), sem("k_lo")
        v_mm, v_hi, v_lo = sem("v_mm"), sem("v_hi"), sem("v_lo")
        s_mm = sem("s_mm")
        s_masked = sem("s_masked")
        max_ok = sem("max_ok")
        shifted = sem("shifted")
        exp_ok = sem("exp_ok")
        sum_ok = sem("sum_ok")
        inv_ok = sem("inv_ok")
        norm_ok = sem("norm_ok")
        p_hi, p_lo = sem("p_hi"), sem("p_lo")
        pT_mm, pT_ok = sem("pT_mm"), sem("pT_ok")
        av_mm, av_hi, av_lo = sem("av_mm"), sem("av_hi"), sem("av_lo")
        y_mm, y_ok = sem("y_mm"), sem("y_ok")
        ffw_int, ffw_ok = sem("ffw_int"), sem("ffw_ok")
        row_ok = sem("row_ok")
        f_mm = sem("f_mm")
        f_scaled, xb_ok, xr_ok = sem("f_scaled"), sem("xb_ok"), sem("xr_ok")
        out_pool, out_dve = sem("out_pool"), sem("out_dve")

        def wait(eng, s, count):
            if not isinstance(count, int) or count > 0:
                eng.wait_ge(s, count)

        def groups(eng, step):
            for tb in range(BLOCKS):
                step(0, tb, True, False)
            with eng.Fori(1, GROUPS - 1) as g:
                for tb in range(BLOCKS):
                    step(g, tb, False, False)
            for tb in range(BLOCKS):
                step(GROUPS - 1, tb, False, True)

        def following(g, tb):
            return (g, tb + 1, 4 * g + tb + 1) if tb + 1 < BLOCKS else (g + 1, 0, 4 * g + BLOCKS)

        def scales(g):
            return g + 3

        def ln_tiles(tb, first, last):
            if first and tb < 2:
                return (tb + 2) * TILES
            return (BLOCKS + tb - 1) * TILES if last and tb > 0 else None

        def ffn_bank(t):
            return (py if t < TILES else pa)[t % 2]

        def toks(tb):
            return slice(tb * BT, (tb + 1) * BT)

        block = stack.enter_context(nc.Block())

        @block.sync
        def _(sp):
            def load_x(tb):
                sp.dma_start(xacc[:, tb * TILES:(tb + 1) * TILES, :],
                             x[tb * TILES:(tb + 1) * TILES].rearrange("t p d -> p t d")).then_inc(x_ld[tb], 16)

            def load_ctx(tb):
                wait(sp, c_scaled, KC * (tb - 1))
                wait(sp, c_lo, KC * (tb - 1))
                sp.dma_start(c_raw[:, tb % 2, :], ctxT[tb]).then_inc(c_ld[tb], 16)

            def load_q(g):
                sp.dma_start(raw_q[:, :, :, :],
                             wqT[g].rearrange("p (h k n) -> p h k n", h=HPG, k=KC)).then_inc(wq_ld, 16)

            def load_kv(g):
                sp.dma_start(raw_k[:, :, :], wkT[g].rearrange("p (k n) -> p k n", k=KC)).then_inc(wkv_ld, 16)
                sp.dma_start(raw_v[:, :, :], wvT[g].rearrange("p (k n) -> p k n", k=KC)).then_inc(wkv_ld, 16)

            def load_d(g):
                sp.dma_start(raw_d[:, :, :], wdT[g].rearrange("p (h n) -> p h n", h=HPG)).then_inc(wd_ld, 16)

            def duplicate_v(m, par):
                sp.wait_ge(v_hi, m + 1)
                sp.wait_ge(v_lo, m + 1)
                for half in range(2):
                    for src in range(2):
                        sp.dma_start(v_dup[half * S:(half + 1) * S, par, src::2, :, :],
                                     v_nat[src * S:(src + 1) * S, :, :, :]).then_inc(v_dup_ld[par], 16)

            for t in range(TILES):
                sp.dma_start(xacc[:, t, :], x[t]).then_inc(x0_ld[t], 16)
            for h in range(HPG):
                sp.dma_start(raw_q[:, h, :, :],
                             wqT[0][:, h * D:(h + 1) * D].rearrange("p (k n) -> p k n", k=KC)).then_inc(wq0_ld[h], 16)
            load_x(1)
            load_ctx(0)
            load_kv(0)
            load_d(0)
            sp.dma_start(gates[:, 0:1], g_x.partition_broadcast(P)).then_inc(g_ld, 16)
            sp.dma_start(gates[:, 1:2], g_f.partition_broadcast(P)).then_inc(g_ld, 16)
            load_ctx(1)
            load_x(2)
            load_x(3)
            load_ctx(2)
            duplicate_v(0, 0)
            load_ctx(3)

            def step(g, tb, first, last):
                _, tbm, m = following(g, tb)
                if not last and tb == 0:
                    sp.wait_ge(wq_hi, 4 * (g + 1))
                    sp.wait_ge(wq_lo, 4 * (g + 1))
                    sp.wait_ge(wk_hi, g + 1)
                    sp.wait_ge(wk_lo, g + 1)
                    sp.wait_ge(wv_hi, g + 1)
                    sp.wait_ge(wv_lo, g + 1)
                    load_q(g + 1)
                    load_kv(g + 1)
                    sp.wait_ge(wd_hi, 4 * (g + 1))
                    sp.wait_ge(wd_lo, 4 * (g + 1))
                    load_d(g + 1)
                if last and tb == 0:
                    sp.wait_ge(c_scaled, KC * BLOCKS)
                    sp.wait_ge(c_lo, KC * BLOCKS)
                    sp.dma_start(ff_raw, qw.rearrange("c p n -> p c n")).then_inc(ff_ld, 16)
                    sp.dma_start(ff_rows[:, ZERO_ROW, :], w_zero.partition_broadcast(P)).then_inc(ff_ld, 16)
                    sp.dma_start(ff_rows[:, SCALE_ROW, :], w_scale.partition_broadcast(P)).then_inc(ff_ld, 16)
                    sp.dma_start(ff_rows[:, BIAS_ROW, :], bias.partition_broadcast(P)).then_inc(ff_ld, 16)
                if not (last and tb == BLOCKS - 1):
                    duplicate_v(m, tbm % 2)

            def store(tb):
                for t in range(tb * TILES, (tb + 1) * TILES):
                    if t < FFN_POOL_TILES:
                        sp.wait_ge(out_pool, t + 1)
                    else:
                        sp.wait_ge(out_dve, t - FFN_POOL_TILES + 1)
                    sp.dma_start(out[t], xacc[:, t, :]).then_inc(stored, 16)

            groups(sp, step)
            for tb in range(BLOCKS):
                store(tb)
            sp.wait_ge(stored, 16 * BLOCKS * TILES)

        @block.gpsimd
        def _(pool):
            pool.memset(ident[:, :], 0.0).then_inc(const_0, 1)
            pool.memset(mask[:, :, :], 0.0).then_inc(const_0, 1)
            pool.wait_ge(const_0, 2)
            pool.affine_select(out=ident[:, :], in_=ident[:, :], compare_op=ALU.not_equal, fill=1.0, base=0,
                               pattern=[[-1, P]], channel_multiplier=1).then_inc(const_ok, 1)
            for half in range(2):
                pool.wait_ge(const_ok, half + 1)
                rows = mask[half * S:(half + 1) * S, 0, :]
                pool.affine_select(out=rows, in_=rows, compare_op=ALU.is_ge, fill=MASKED, base=0,
                                   pattern=[[-1, S]], channel_multiplier=1).then_inc(const_ok, 1)

            def reduce_ctx(tb):
                pool.wait_ge(c_max_ok, tb + 1)
                pool.partition_all_reduce(c_all[:, tb:tb + 1], c_max[:, tb:tb + 1], P,
                                          bass.bass_isa.ReduceOp.max).then_inc(c_red_ok, 1)

            def reduce_w(maxima, cols):
                pool.wait_ge(w_max_ok, maxima)
                pool.sem_inc(w_max_seen, 1)
                pool.partition_all_reduce(w_all[:, cols], w_max[:, cols], P,
                                          bass.bass_isa.ReduceOp.max).then_inc(w_red_ok, 1)

            def ctx_lo(tb, chunks=range(KC)):
                for kc in chunks:
                    pool.wait_ge(c_scaled, KC * tb + kc + 1)
                    pool.tensor_tensor(cT[:, LO, kc, toks(tb)], c_raw[:, tb % 2, kc * BT:(kc + 1) * BT],
                                       cT[:, HI, kc, toks(tb)], ALU.subtract).then_inc(c_lo, 1)

            def ln_lo(t):
                pool.wait_ge(x_hi, t + 1)
                pool.tensor_tensor(xh[:, t % SLOTS, LO, :], xn[:, t % SLOTS, :], xh[:, t % SLOTS, HI, :],
                                   ALU.subtract).then_inc(x_lo, 1)

            def ln_rstd(call):
                pool.wait_ge(seed_ok, 4 * (call + 1))
                count = 12 * call

                def chained(ins):
                    nonlocal count
                    count += 1
                    ins.then_inc(rs_ok, 1)
                    pool.wait_ge(rs_ok, count)

                for i in range(3):
                    y = rs[:, i, :]
                    chained(pool.tensor_tensor(rs_t[:, :], y, y, ALU.mult))
                    chained(pool.tensor_tensor(rs_t[:, :], rs_t[:, :], half_var[:, :], ALU.mult))
                    chained(pool.tensor_scalar(rs_t[:, :], rs_t[:, :], 1.5, 1.0 if i < 2 else XN_SCALE,
                                               ALU.add, ALU.mult))
                    chained(pool.tensor_tensor(rs[:, i + 1, :] if i < 2 else rstd[:, :], rs_t[:, :], y, ALU.mult))

            def residual(t):
                if t == 0:
                    pool.wait_ge(row_ok, 3)
                pool.wait_ge(xn_ok, BLOCKS * TILES + t + 1)
                pool.tensor_tensor(xacc[:, t, :], xacc[:, t, :], ff_rows[:, BIAS_ROW, :], ALU.add).then_inc(xb_ok, 1)

            def ffn_add(t):
                pool.wait_ge(xr_ok, t + 1)
                pool.wait_ge(f_scaled, t + 1)
                pool.tensor_tensor(xacc[:, t, :], xacc[:, t, :], xs[t % len(xs)], ALU.add).then_inc(out_pool, 1)

            pool.wait_ge(const_ok, 3)
            ln_rstd(0)
            reduce_w(1, slice(0, 1))
            pool.wait_ge(w_red_ok, 1)
            for t in range(2):
                ln_lo(t)
            pool.wait_ge(x_lo, TILES)
            reduce_ctx(0)
            pool.wait_ge(c_red_ok, 1)
            reduce_w(3, slice(1, 3))
            pool.wait_ge(w_red_ok, 2)
            ctx_lo(0)
            ln_rstd(1)
            pool.wait_ge(c_lo, KC)
            reduce_ctx(1)
            pool.wait_ge(c_red_ok, 2)
            for t in range(TILES):
                ln_lo(TILES + t)
            pool.wait_ge(x_lo, 2 * TILES)
            reduce_w(4, slice(3, 4))
            pool.wait_ge(w_red_ok, 3)
            ctx_lo(1)

            def step(g, tb, first, last):
                ln = ln_tiles(tb, first, last)
                if first and tb in (1, 2):
                    pool.wait_ge(x_lo, (tb + 2) * TILES)
                    reduce_ctx(tb + 1)
                    pool.wait_ge(c_red_ok, tb + 2)
                    ctx_lo(tb + 1)
                if last and tb == BLOCKS - 1:
                    for t in range(TILES):
                        ffn_add(t)
                if ln is not None:
                    ln_rstd(ln // TILES)
                    if last and tb == BLOCKS - 1:
                        for t in range(TILES, 2 * TILES):
                            ffn_add(t)
                    for t in range(TILES):
                        ln_lo(ln + t)
                if not last and tb == 1:
                    if first:
                        pool.wait_ge(x_lo, BLOCKS * TILES)
                    reduce_w(4 * (g + 2), slice(0, 4))
                if last and tb > 0:
                    for t in range((tb - 1) * TILES, tb * TILES):
                        if t == (BLOCKS - 1) * TILES - 2:
                            ln_rstd(2 * BLOCKS - 1)
                        residual(t)

            groups(pool, step)
            for t in range((BLOCKS - 1) * TILES, BLOCKS * TILES):
                residual(t)
            for t in range((BLOCKS - 2) * TILES, FFN_POOL_TILES):
                ffn_add(t)

        @block.scalar
        def _(act):
            def split_ctx(tb, chunks=range(KC)):
                if 0 in chunks:
                    act.wait_ge(c_ld[tb], 16)
                    act.wait_ge(c_mul_ok, tb + 1)
                for kc in chunks:
                    part = c_raw[:, tb % 2, kc * BT:(kc + 1) * BT]
                    act.activation(cT[:, HI, kc, toks(tb)], part, ACT.Copy, scale=c_mul[:, tb:tb + 1]).then_inc(c_hi, 1)
                    act.activation(part, part, ACT.Copy, scale=c_mul[:, tb:tb + 1]).then_inc(c_scaled, 1)

            def split_wq(g, h):
                if h == 0:
                    act.wait_ge(w_mul_ok, scales(g) if not isinstance(g, int) or g > 0 else 1)
                act.activation(wq[:, HI, h, :, :], raw_q[:, h, :, :], ACT.Copy,
                               scale=w_mul[:, 0:1]).then_inc(wq_hi, 1)

            def split_wk(g, count):
                act.wait_ge(w_mul_ok, count)
                act.activation(wk[:, HI, :, :], raw_k[:, :, :], ACT.Copy, scale=w_mul[:, 1:2]).then_inc(wk_hi, 1)

            def split_wv(g):
                act.activation(wv[:, HI, :, :], raw_v[:, :, :], ACT.Copy, scale=w_mul[:, 2:3]).then_inc(wv_hi, 1)

            def split_wd(g):
                wait(act, y_mm, 16 * g)
                for h in range(HPG):
                    act.activation(wd[:, HI, h, :], raw_d[:, h, :], ACT.Copy, scale=w_mul[:, 3:4]).then_inc(wd_hi, 1)

            def q_part(m, h):
                act.wait_ge(q_mm, 4 * m + h + 1)
                act.activation(q[:, HI, :, h, :], pa[h % 2][:, :].rearrange("p (b s) -> p b s", b=BPB), ACT.Copy,
                               scale=Q_SCALE).then_inc(q_hi, 1)

            def k_part(m):
                act.wait_ge(k_mm, m + 1)
                act.activation(k[:, HI, :], pa[0][:, :], ACT.Copy, scale=K_SCALE).then_inc(k_hi, 1)

            def v_part(m, par):
                act.wait_ge(v_mm, m + 1)
                wait(act, v_dup_ld[1 - par], 32 * (m + par))
                act.activation(v_nat[:, :, HI, :], pa[1][:, :].rearrange("p (t n) -> p t n", t=TILES), ACT.Copy,
                               scale=K_SCALE).then_inc(v_hi, 1)

            def ln_hi(t, summed):
                act.wait_ge(xn_ok, t + 1)
                wait(act, xT_mm, t - SLOTS + 1)
                at = t - BLOCKS * TILES
                act.activation(xh[:, t % SLOTS, HI, :], xn[:, t % SLOTS, :], ACT.Copy,
                               accum_out=x_sum[:, at:at + 1] if summed else None).then_inc(x_hi, 1)

            def ln_out(t):
                act.wait_ge(xT_mm, t + 1)
                at = t % (BLOCKS * TILES) * P
                act.copy(xT[:, :, :, at:at + P],
                         av[t % 2][:, :].bitcast(F16).rearrange("p (c k n) -> p c k n", c=2, k=KC)).then_inc(xT_ok, 1)

            def exp(n, p):
                act.wait_ge(shifted, 2 * n + p + 1)
                act.activation(sc[:, p, :, :], sc[:, p, :, :], ACT.Exp).then_inc(exp_ok, 1)

            def p_part(n, p):
                act.wait_ge(norm_ok, 2 * n + p + 1)
                act.copy(pr[:, p, :, HI, :], sc[:, p, :, :]).then_inc(p_hi, 1)

            def p_transposed(n, p):
                act.wait_ge(pT_mm, 2 * n + p + 1)
                act.copy(pT[:, :, 2 * p:2 * p + 2, :],
                         pp[:, :].bitcast(F16).rearrange("p (b e s) -> p b e s", b=BPB, e=2)).then_inc(pT_ok, 1)

            def av_part(n, j):
                act.wait_ge(av_mm, 4 * n + j + 1)
                for bb in range(2):
                    at = (2 * j + bb) * S
                    last = act.activation(att[:, HI, :, at:at + S],
                                          av[j % 2][:, bb * 256:(bb + 1) * 256].rearrange("p (h s) -> p h s", h=HPG),
                                          ACT.Copy, scale=AV_SCALE)
                last.then_inc(av_hi, 1)

            for t in range(SLOTS):
                ln_hi(t, False)
            ln_out(0)
            ln_hi(SLOTS, False)
            for t in range(1, TILES):
                ln_out(t)
            act.wait_ge(wq_hi, 2)
            for h in range(2, HPG):
                split_wq(0, h)
            q_part(0, 0)
            split_ctx(0, (0, 1))
            q_part(0, 1)
            split_wk(0, 2)
            split_wv(0)
            q_part(0, 2)
            split_ctx(0, (2, 3))
            q_part(0, 3)
            k_part(0)
            for t in range(SLOTS):
                ln_hi(TILES + t, False)
            v_part(0, 0)
            ln_out(TILES)
            ln_hi(TILES + SLOTS, False)
            ln_out(TILES + 1)
            ln_out(TILES + 2)
            ln_out(TILES + 3)
            act.wait_ge(g_ld, 32)
            act.activation(tg[:, :], gates[:, :], ACT.Tanh).then_inc(tanh_ok, 1)
            split_ctx(1)

            def step(g, tb, first, last):
                n = 4 * g + tb
                gm, tbm, m = following(g, tb)
                ahead = not (last and tb == BLOCKS - 1)
                reweigh = tb == 2 and not last
                ln = ln_tiles(tb, first, last)
                if ahead:
                    q_part(m, 0)
                exp(n, 0)
                if tb == 0:
                    if first:
                        act.wait_ge(w_mul_ok, scales(0))
                    else:
                        act.wait_ge(wd_ld, 16 * (g + 1))
                    split_wd(g)
                if first and tb in (1, 2):
                    split_ctx(tb + 1, (0, 1))
                if ahead:
                    q_part(m, 1)
                p_part(n, 0)
                exp(n, 1)
                if ahead:
                    q_part(m, 2)
                if first and tb in (1, 2):
                    split_ctx(tb + 1, (2, 3))
                p_part(n, 1)
                if ahead:
                    q_part(m, 3)
                p_transposed(n, 0)
                if ahead:
                    k_part(m)
                p_transposed(n, 1)
                av_part(n, 0)
                av_part(n, 1)
                if ahead:
                    v_part(m, tbm % 2)
                av_part(n, 2)
                if reweigh:
                    for h in range(HPG):
                        split_wq(g + 1, h)
                av_part(n, 3)
                if ln is not None:
                    for t in range(SLOTS):
                        ln_hi(ln + t, last)
                    ln_out(ln)
                    ln_hi(ln + SLOTS, last)
                    for t in range(1, TILES):
                        ln_out(ln + t)
                if reweigh:
                    split_wk(g + 1, scales(g + 1))
                    split_wv(g + 1)

            groups(act, step)
            t0 = (2 * BLOCKS - 1) * TILES
            for t in range(SLOTS):
                ln_hi(t0 + t, True)
            ln_out(t0)
            ln_hi(t0 + SLOTS, True)
            for t in range(1, TILES):
                ln_out(t0 + t)

        @block.vector
        def _(dve):
            def power_of_two(raw, guarded, pow2, inverse, factor, cols, red_ok, grd_ok, pow_ok, inv_ok_, mul_ok, count):
                dve.wait_ge(red_ok, count)
                dve.tensor_scalar(guarded[:, cols], raw[:, cols], 1e-30, None, ALU.max).then_inc(grd_ok, 1)
                dve.wait_ge(grd_ok, count)
                dve.tensor_scalar(pow2[:, cols].bitcast(I32), guarded[:, cols].bitcast(I32), EXPONENT, None,
                                  ALU.bitwise_and).then_inc(pow_ok, 1)
                dve.wait_ge(pow_ok, count)
                dve.reciprocal(inverse[:, cols], pow2[:, cols]).then_inc(inv_ok_, 1)
                dve.wait_ge(inv_ok_, count)
                dve.tensor_scalar(factor[:, cols], inverse[:, cols], W_SCALE, None, ALU.mult).then_inc(mul_ok, 1)

            def ctx_max(tb):
                dve.wait_ge(c_ld[tb], 16)
                dve.tensor_reduce(c_max[:, tb:tb + 1], c_raw[:, tb % 2, :], AX.X, ALU.max,
                                  apply_absolute_value=True).then_inc(c_max_ok, 1)

            def ctx_scale(tb):
                power_of_two(c_all, c_grd, c_pow, c_inv, c_mul, slice(tb, tb + 1),
                             c_red_ok, c_grd_ok, c_pow_ok, c_inv_ok, c_mul_ok, tb + 1)

            def weight_max(g, which):
                if 0 in which:
                    dve.wait_ge(wq_ld, 16 * g)
                if 1 in which:
                    dve.wait_ge(wkv_ld, 32 * (g + 1))
                for i, raw in enumerate((raw_q[:, :, :, :].rearrange("p h k n -> p (h k n)"),
                                         raw_k[:, :, :].rearrange("p k n -> p (k n)"),
                                         raw_v[:, :, :].rearrange("p k n -> p (k n)"),
                                         raw_d[:, :, :].rearrange("p h n -> p (h n)"))):
                    if i not in which:
                        continue
                    if i == 3:
                        dve.wait_ge(wd_ld, 16 * (g + 1))
                    dve.tensor_reduce(w_max[:, i:i + 1], raw, AX.X, ALU.max,
                                      apply_absolute_value=True).then_inc(w_max_ok, 1)

            def first_wq_max():
                for h in range(HPG):
                    dve.wait_ge(wq0_ld[h], 16)
                    dve.tensor_reduce(head_max[:, h:h + 1], raw_q[:, h, :, :].rearrange("p k n -> p (k n)"), AX.X,
                                      ALU.max, apply_absolute_value=True).then_inc(head_max_ok, 1)
                dve.wait_ge(head_max_ok, HPG)
                dve.tensor_reduce(w_max[:, 0:1], head_max[:, :], AX.X, ALU.max).then_inc(w_max_ok, 1)

            def weight_scale(g, cols, count):
                power_of_two(w_all, w_grd, w_pow, w_inv, w_mul, cols,
                             w_red_ok, w_grd_ok, w_pow_ok, w_inv_ok, w_mul_ok, count)

            def weight_products(g, count):
                for i in range(2):
                    dve.tensor_tensor(w_prod[:, i:i + 1], w_pow[:, 2 * i:2 * i + 1], w_pow[:, 2 * i + 1:2 * i + 2],
                                      ALU.mult).then_inc(w_prod_ok, 1)
                dve.wait_ge(w_mul_ok, count)

            def unscale(g, cols, count):
                if cols.start == 0:
                    dve.wait_ge(w_prod_ok, 2 * (g + 1))
                    dve.tensor_copy(w_now[:, :], w_prod[:, :]).then_inc(w_now_ok, 1)
                    dve.wait_ge(w_now_ok, g + 1)
                dve.tensor_scalar(f_score[:, cols], c_pow[:, cols], w_now[:, 0:1], SCORE_UNSCALE,
                                  ALU.mult, ALU.mult).then_inc(f_ok, 1)
                wait(dve, y_ok, 16 * g)
                dve.tensor_scalar(f_y[:, cols], c_pow[:, cols], w_now[:, 1:2], tgy[:, 0:1],
                                  ALU.mult, ALU.mult).then_inc(f_ok, 1)
                dve.wait_ge(f_ok, count)

            def lo_part(out, in0, scale, hi, done):
                dve.scalar_tensor_tensor(out=out, in0=in0, scalar=scale, in1=hi,
                                         op0=ALU.mult, op1=ALU.subtract).then_inc(done, 1)

            def split_wq(g, h):
                dve.wait_ge(wq_hi, 4 * g + h + 1)
                lo_part(wq[:, LO, h, :, :], raw_q[:, h, :, :], w_mul[:, 0:1], wq[:, HI, h, :, :], wq_lo)

            def split_wk(g):
                dve.wait_ge(wk_hi, g + 1)
                lo_part(wk[:, LO, :, :], raw_k[:, :, :], w_mul[:, 1:2], wk[:, HI, :, :], wk_lo)

            def split_wv(g):
                dve.wait_ge(wv_hi, g + 1)
                lo_part(wv[:, LO, :, :], raw_v[:, :, :], w_mul[:, 2:3], wv[:, HI, :, :], wv_lo)

            def split_wd(g):
                for h in range(HPG):
                    dve.wait_ge(wd_hi, 4 * g + h + 1)
                    lo_part(wd[:, LO, h, :], raw_d[:, h, :], w_mul[:, 3:4], wd[:, HI, h, :], wd_lo)

            def q_part(m, h):
                dve.wait_ge(q_hi, 4 * m + h + 1)
                lo_part(q[:, LO, :, h, :], pa[h % 2][:, :].rearrange("p (b s) -> p b s", b=BPB), Q_SCALE,
                        q[:, HI, :, h, :], q_lo)

            def k_part(m):
                dve.wait_ge(k_hi, m + 1)
                lo_part(k[:, LO, :], pa[0][:, :], K_SCALE, k[:, HI, :], k_lo)

            def v_part(m):
                dve.wait_ge(v_hi, m + 1)
                lo_part(v_nat[:, :, LO, :], pa[1][:, :].rearrange("p (t n) -> p t n", t=TILES), K_SCALE,
                        v_nat[:, :, HI, :], v_lo)

            def scores(n, tb, p):
                dve.wait_ge(s_mm, 2 * n + p + 1)
                dve.scalar_tensor_tensor(out=sc[:, p, :, :], in0=ps[:, :].rearrange("p (b s) -> p b s", b=BPB),
                                         scalar=f_score[:, tb:tb + 1], in1=mask[:, :, :].to_broadcast([P, BPB, S]),
                                         op0=ALU.mult, op1=ALU.add).then_inc(s_masked, 1)
                dve.wait_ge(s_masked, 2 * n + p + 1)
                dve.tensor_reduce(row_max[:, p, :], sc[:, p, :, :], AX.X, ALU.max).then_inc(max_ok, 1)
                dve.wait_ge(max_ok, 2 * n + p + 1)
                dve.tensor_tensor(sc[:, p, :, :], sc[:, p, :, :],
                                  row_max[:, p, :].unsqueeze(2).to_broadcast([P, BPB, S]),
                                  ALU.subtract).then_inc(shifted, 1)

            def normalise(n, p):
                dve.wait_ge(exp_ok, 2 * n + p + 1)
                dve.tensor_reduce(row_sum[:, p, :], sc[:, p, :, :], AX.X, ALU.add).then_inc(sum_ok, 1)
                dve.wait_ge(sum_ok, 2 * n + p + 1)
                dve.reciprocal(row_inv[:, p, :], row_sum[:, p, :]).then_inc(inv_ok, 1)
                dve.wait_ge(inv_ok, 2 * n + p + 1)
                dve.scalar_tensor_tensor(out=sc[:, p, :, :], in0=sc[:, p, :, :], scalar=P_SCALE,
                                         in1=row_inv[:, p, :].unsqueeze(2).to_broadcast([P, BPB, S]),
                                         op0=ALU.mult, op1=ALU.mult).then_inc(norm_ok, 1)

            def p_part(n, p):
                dve.wait_ge(p_hi, 2 * n + p + 1)
                dve.tensor_tensor(pr[:, p, :, LO, :], sc[:, p, :, :], pr[:, p, :, HI, :],
                                  ALU.subtract).then_inc(p_lo, 1)

            def av_part(n, j):
                dve.wait_ge(av_hi, 4 * n + j + 1)
                for bb in range(2):
                    at = (2 * j + bb) * S
                    last = dve.scalar_tensor_tensor(
                        out=att[:, LO, :, at:at + S],
                        in0=av[j % 2][:, bb * 256:(bb + 1) * 256].rearrange("p (h s) -> p h s", h=HPG),
                        scalar=AV_SCALE, in1=att[:, HI, :, at:at + S], op0=ALU.mult, op1=ALU.subtract)
                last.then_inc(av_lo, 1)

            def y_part(n, tb, j):
                dve.wait_ge(y_mm, 4 * n + j + 1)
                t = tb * TILES + j
                dve.scalar_tensor_tensor(out=xacc[:, t, :], in0=py[j % 2][:, :], scalar=f_y[:, tb:tb + 1],
                                         in1=xacc[:, t, :], op0=ALU.mult, op1=ALU.add).then_inc(y_ok, 1)

            def ln_bn(tb, t, second):
                if second:
                    dve.wait_ge(y_ok, 4 * (BLOCKS * (GROUPS - 1) + tb) + t + 1)
                elif tb == 0:
                    dve.wait_ge(x0_ld[t], 16)
                else:
                    dve.wait_ge(x_ld[tb], 16)
                dve.bn_stats(bn[:, t, :], xacc[:, tb * TILES + t, :]).then_inc(bn_ok, 1)

            def ln_stats(tb, second):
                call = tb + (BLOCKS if second else 0)
                for t in range(TILES):
                    dve.wait_ge(bn_ok, TILES * call + t + 1)
                    dve.bn_aggr(mv[:, t, :], bn[:, t, :]).then_inc(mv_ok, 1)
                dve.wait_ge(mv_ok, TILES * (call + 1))
                dve.tensor_scalar(var_e[:, :], mv[:, :, 1], LN_EPS, None, ALU.add).then_inc(seed_ok, 1)
                dve.tensor_scalar(half_var[:, :], mv[:, :, 1], LN_EPS, -0.5, ALU.add, ALU.mult).then_inc(seed_ok, 1)
                dve.wait_ge(seed_ok, 4 * call + 2)
                dve.tensor_scalar(rs_bits[:, :], var_e[:, :].bitcast(I32), 1, None,
                                  ALU.logical_shift_right).then_inc(seed_ok, 1)
                dve.wait_ge(seed_ok, 4 * call + 3)
                dve.tensor_scalar(rs[:, 0, :].bitcast(I32), rs_bits[:, :], -1.0, float(RSQRT_MAGIC),
                                  ALU.mult, ALU.add).then_inc(seed_ok, 1)

            def ln_norm(t):
                dve.wait_ge(rs_ok, 12 * (t // TILES + 1))
                wait(dve, x_lo, t - SLOTS + 1)
                at = t % TILES
                dve.tensor_scalar(xn[:, t % SLOTS, :], xacc[:, t % (BLOCKS * TILES), :], mv[:, at, 0:1],
                                  rstd[:, at:at + 1], ALU.subtract, ALU.mult).then_inc(xn_ok, 1)

            def ln_lo(t):
                dve.wait_ge(x_hi, t + 1)
                dve.wait_ge(x_lo, t)
                dve.wait_ge(xn_ok, t + 1)
                dve.tensor_tensor(xh[:, t % SLOTS, LO, :], xn[:, t % SLOTS, :], xh[:, t % SLOTS, HI, :],
                                  ALU.subtract).then_inc(x_lo, 1)

            def ffn_weight(j):
                if j == 0:
                    dve.wait_ge(ff_ld, 64)
                word, shift = ((0, 0), (0, 6), (1, 0), (2, 0))[j]
                dve.tensor_scalar(xn[:, j % 2, :].bitcast(I32), ff_raw[:, word, :], shift, 63,
                                  ALU.logical_shift_right, ALU.bitwise_and).then_inc(ffw_int, 1)
                dve.wait_ge(ffw_int, j + 1)
                dve.tensor_copy(ff_w[:, j, :], xn[:, j % 2, :].bitcast(I32)).then_inc(ffw_ok, 1)

            def ffn_rows():
                dve.tensor_scalar(ff_rows[:, SCALE_ROW, :], ff_rows[:, SCALE_ROW, :], tg[:, 1:2], 1.0 / XN_SCALE,
                                  ALU.mult, ALU.mult).then_inc(row_ok, 1)
                dve.tensor_scalar(ff_rows[:, BIAS_ROW, :], ff_rows[:, BIAS_ROW, :], tg[:, 1:2], None,
                                  ALU.mult).then_inc(row_ok, 1)
                dve.wait_ge(row_ok, 1)
                dve.scalar_tensor_tensor(out=ff_rows[:, ZERO_ROW, :], in0=ff_rows[:, ZERO_ROW, :], scalar=-1.0,
                                         in1=ff_rows[:, SCALE_ROW, :], op0=ALU.mult, op1=ALU.mult).then_inc(row_ok, 1)
                dve.wait_ge(row_ok, 3)

            def ffn_zero(t):
                dve.wait_ge(xb_ok, t + 1)
                dve.wait_ge(x_hi, BLOCKS * TILES + t + 1)
                dve.scalar_tensor_tensor(out=xacc[:, t, :], in0=ff_rows[:, ZERO_ROW, :], scalar=x_sum[:, t:t + 1],
                                         in1=xacc[:, t, :], op0=ALU.mult, op1=ALU.add).then_inc(xr_ok, 1)

            def ffn_scaled(t):
                wait(dve, out_pool, t - len(xs) + 1)
                dve.wait_ge(f_mm, t + 1)
                dve.tensor_tensor(xs[t % len(xs)], ffn_bank(t)[:, :], ff_rows[:, SCALE_ROW, :],
                                  ALU.mult).then_inc(f_scaled, 1)

            def wq_high(h):
                dve.tensor_scalar(wq[:, HI, h, :, :], raw_q[:, h, :, :], w_mul[:, 0:1], None,
                                  ALU.mult).then_inc(wq_hi, 1)

            def ffn_result(t):
                dve.wait_ge(xr_ok, t + 1)
                dve.wait_ge(f_scaled, t + 1)
                dve.tensor_tensor(xacc[:, t, :], xacc[:, t, :], xs[t % len(xs)], ALU.add).then_inc(out_dve, 1)

            for t in range(TILES):
                ln_bn(0, t, False)
            ln_stats(0, False)
            first_wq_max()
            for t in range(SLOTS):
                ln_norm(t)
            weight_scale(0, slice(0, 1), 1)
            dve.wait_ge(w_mul_ok, 1)
            wq_high(0)
            ln_norm(SLOTS)
            wq_high(1)
            ln_lo(2)
            ln_lo(3)
            split_wq(0, 0)
            split_wq(0, 1)
            ctx_max(0)
            split_wq(0, 2)
            ctx_scale(0)
            weight_max(0, (1, 2))
            q_part(0, 0)
            split_wq(0, 3)
            weight_scale(0, slice(1, 3), 2)
            q_part(0, 1)
            for t in range(2):
                ln_bn(1, t, False)
            split_wk(0)
            q_part(0, 2)
            for t in range(2, TILES):
                ln_bn(1, t, False)
            ln_stats(1, False)
            split_wv(0)
            q_part(0, 3)
            ctx_max(1)
            k_part(0)
            for t in range(SLOTS):
                ln_norm(TILES + t)
            ctx_scale(1)
            v_part(0)
            ln_norm(TILES + SLOTS)
            weight_max(0, (3,))
            weight_scale(0, slice(3, 4), 3)
            weight_products(0, 3)
            dve.wait_ge(tanh_ok, 1)
            dve.tensor_scalar(tgy[:, :], tg[:, 0:1], Y_UNSCALE, None, ALU.mult).then_inc(tgy_ok, 1)
            dve.wait_ge(tgy_ok, 1)

            def step(g, tb, first, last):
                n = 4 * g + tb
                gm, tbm, m = following(g, tb)
                ahead = not (last and tb == BLOCKS - 1)
                reweigh = tb == 2 and not last
                ln = ln_tiles(tb, first, last)
                final = last and tb == BLOCKS - 1
                if first:
                    if tb == 0:
                        dve.wait_ge(const_ok, 3)
                    unscale(g, slice(tb, tb + 1), 2 * (tb + 1))
                elif tb == 0:
                    unscale(g, slice(0, BLOCKS), 2 * BLOCKS + 2 * g)
                scores(n, tb, 0)
                if first and tb in (1, 2):
                    ctx_scale(tb + 1)
                if first and tb < 2:
                    for t in range(TILES):
                        ln_bn(tb + 2, t, False)
                if final:
                    ffn_scaled(0)
                    ffn_scaled(1)
                if ahead:
                    q_part(m, 0)
                scores(n, tb, 1)
                normalise(n, 0)
                if final:
                    ffn_scaled(2)
                if ahead:
                    q_part(m, 1)
                p_part(n, 0)
                normalise(n, 1)
                if final:
                    ffn_scaled(3)
                if ahead:
                    q_part(m, 2)
                p_part(n, 1)
                if reweigh:
                    weight_scale(g + 1, slice(0, 4), scales(g + 1))
                    weight_products(g + 1, scales(g + 1))
                if ahead:
                    q_part(m, 3)
                if tb == 0:
                    split_wd(g)
                if first and tb == 1:
                    ctx_max(3)
                if ahead:
                    k_part(m)
                if final:
                    ffn_scaled(4)
                if ln is not None:
                    ln_stats(ln // TILES % BLOCKS, last)
                if final:
                    ffn_scaled(5)
                    ffn_scaled(6)
                av_part(n, 0)
                if final:
                    ffn_scaled(7)
                av_part(n, 1)
                if final:
                    for t in range(TILES, 2 * TILES):
                        ffn_zero(t)
                if ahead:
                    v_part(m)
                if last and tb == 1:
                    ffn_rows()
                for j in range(TILES):
                    y_part(n, tb, j)
                    if last:
                        ln_bn(tb, j, True)
                    if j < 2:
                        av_part(n, j + 2)
                    if ln is not None and j == 0:
                        for t in range(SLOTS):
                            ln_norm(ln + t)
                    if ln is not None and j == 1:
                        ln_norm(ln + SLOTS)
                    if first and tb == 0 and j == 2:
                        ctx_max(2)
                    if last and tb == 0:
                        ffn_weight(j)
                    if last and tb == 2:
                        ffn_zero(j)
                    if tb == 1 and not last:
                        weight_max(g + 1, ((0,), (1, 2), (3,), ())[j])
                    if reweigh:
                        if j < 2:
                            split_wq(g + 1, 2 * j)
                            split_wq(g + 1, 2 * j + 1)
                        elif j == 2:
                            split_wk(g + 1)
                            split_wv(g + 1)

            groups(dve, step)
            ln_stats(BLOCKS - 1, True)
            t0 = (BLOCKS - 1) * TILES
            ffn_scaled(t0 - TILES)
            ffn_scaled(t0 - TILES + 1)
            ln0 = BLOCKS * TILES + t0
            for t in range(SLOTS):
                ln_norm(ln0 + t)
            ln_lo(ln0)
            ln_lo(ln0 + 1)
            ln_norm(ln0 + SLOTS)
            ffn_scaled(t0 - TILES + 2)
            ffn_scaled(t0 - TILES + 3)
            ln_lo(ln0 + 2)
            ffn_zero(t0 - TILES)
            ln_lo(ln0 + 3)
            ffn_zero(t0 - 3)
            ffn_scaled(t0)
            ffn_zero(t0 - 2)
            ffn_scaled(t0 + 1)
            for t in range(t0 - 1, t0 + 2):
                ffn_zero(t)
            for t in range(t0 + 2, t0 + TILES):
                ffn_zero(t)
                if t > FFN_POOL_TILES:
                    ffn_result(t - 1)
                ffn_scaled(t)
            ffn_result(BLOCKS * TILES - 1)

        @block.tensor
        def _(pe):
            def product(out, stationary, moving, count, ready=None):
                for i in range(count):
                    if ready:
                        ready(i)
                    for a, b in PASSES:
                        last = pe.matmul(out, stationary(a, i), moving(b, i),
                                         start=(i == 0 and (a, b) == PASSES[0]),
                                         stop=(i == count - 1 and (a, b) == PASSES[-1]))
                return last

            def q_unit(gm, tbm, m, h, in_first):
                pe.wait_ge(wq_hi, 4 * gm + h + 1)
                pe.wait_ge(wq_lo, 4 * gm + h + 1)
                if h == 0:
                    if in_first:
                        pe.wait_ge(xT_ok, TILES * (tbm + 1))
                    wait(pe, k_hi, m)
                    wait(pe, k_lo, m)
                elif h == 1:
                    wait(pe, v_hi, m)
                    wait(pe, v_lo, m)
                else:
                    pe.wait_ge(q_hi, 4 * m + h - 1)
                    pe.wait_ge(q_lo, 4 * m + h - 1)
                product(pa[h % 2][:, :], lambda a, i: wq[:, a, h, i, :], lambda b, i: xT[:, b, i, toks(tbm)],
                        KC).then_inc(q_mm, 1)

            def k_unit(gm, tbm, m, in_first):
                pe.wait_ge(wk_hi, gm + 1)
                pe.wait_ge(wk_lo, gm + 1)
                pe.wait_ge(q_hi, 4 * m + 3)
                pe.wait_ge(q_lo, 4 * m + 3)

                def chunk(i):
                    if in_first:
                        pe.wait_ge(c_hi, KC * tbm + i + 1)
                        pe.wait_ge(c_lo, KC * tbm + i + 1)

                product(pa[0][:, :], lambda a, i: wk[:, a, i, :], lambda b, i: cT[:, b, i, toks(tbm)],
                        KC, chunk).then_inc(k_mm, 1)

            def v_unit(gm, tbm, m, tiles):
                if 0 in tiles:
                    pe.wait_ge(wv_hi, gm + 1)
                    pe.wait_ge(wv_lo, gm + 1)
                    pe.wait_ge(q_hi, 4 * m + 4)
                    pe.wait_ge(q_lo, 4 * m + 4)
                for t in tiles:
                    at = tbm * BT + t * P
                    last = product(pa[1][:, t * P:(t + 1) * P], lambda a, i: cT[:, a, i, at:at + P],
                                   lambda b, i: wv[:, b, i, :], KC)
                if TILES - 1 in tiles:
                    last.then_inc(v_mm, 1)

            def score_unit(n, p):
                pe.wait_ge(q_hi, 4 * n + 2 * p + 2)
                pe.wait_ge(q_lo, 4 * n + 2 * p + 2)
                if p == 0:
                    pe.wait_ge(k_hi, n + 1)
                    pe.wait_ge(k_lo, n + 1)
                wait(pe, s_masked, 2 * n + p)
                for b in range(BPB):
                    for a, c in PASSES:
                        last = pe.matmul(ps[:, b * S:(b + 1) * S],
                                         q[:, a, b, 2 * p:2 * p + 2, :].rearrange("p e s -> p (e s)"),
                                         k[:, c, b * S:(b + 1) * S],
                                         start=((a, c) == PASSES[0]), stop=((a, c) == PASSES[-1]))
                last.then_inc(s_mm, 1)

            def p_transpose(n, p):
                pe.wait_ge(p_hi, 2 * n + p + 1)
                pe.wait_ge(p_lo, 2 * n + p + 1)
                wait(pe, pT_ok, 2 * n + p)
                bank16 = pp[:, :].bitcast(F16)
                for b in range(BPB):
                    last = pe.transpose(bank16[:, b * P:(b + 1) * P],
                                        pr[:, p, b, :, :].rearrange("p c s -> p (c s)"), ident[:, :])
                last.then_inc(pT_mm, 1)

            def av_unit(n, par, j):
                if j == 0:
                    pe.wait_ge(pT_ok, 2 * n + 2)
                    pe.wait_ge(v_dup_ld[par], 32 * (n + 2 - par))
                wait(pe, av_hi, 4 * n + j - 1)
                wait(pe, av_lo, 4 * n + j - 1)
                for bb in range(2):
                    b = 2 * j + bb
                    for c in (HI, LO):
                        last = pe.matmul(av[j % 2][:, bb * 256:(bb + 1) * 256], v_dup[:, par, b, c, :],
                                         pT[:, b, :, :].rearrange("p h s -> p (h s)"),
                                         start=(c == HI), stop=(c == LO))
                last.then_inc(av_mm, 1)

            def y_unit(g, n, j):
                if j == 0:
                    pe.wait_ge(wd_hi, 4 * (g + 1))
                    pe.wait_ge(wd_lo, 4 * (g + 1))
                pe.wait_ge(av_hi, 4 * n + j + 1)
                pe.wait_ge(av_lo, 4 * n + j + 1)
                wait(pe, y_ok, 4 * n + j - 1)
                product(py[j % 2][:, :], lambda a, h: att[:, a, h, j * P:(j + 1) * P],
                        lambda b, h: wd[:, b, h, :], HPG).then_inc(y_mm, 1)

            def ln_transpose(t, av_before):
                pe.wait_ge(x_hi, t + 1)
                pe.wait_ge(x_lo, t + 1)
                wait(pe, xT_ok, t - 1)
                wait(pe, av_hi, av_before)
                wait(pe, av_lo, av_before)
                bank16 = av[t % 2][:, :].bitcast(F16)
                for c in (HI, LO):
                    for i in range(KC):
                        if t < BLOCKS * TILES:
                            part = xh[:, t % SLOTS, c, i * P:(i + 1) * P]
                        else:
                            part = xh[:, t % SLOTS, c, :].rearrange("p (i j) -> p j i", j=KC)[:, i, :]
                        at = (c * KC + i) * P
                        last = pe.transpose(bank16[:, at:at + P], part, ident[:, :])
                last.then_inc(xT_mm, 1)

            def ffn_unit(t, n):
                if t == 0:
                    pe.wait_ge(ffw_ok, 4)
                pe.wait_ge(xT_ok, BLOCKS * TILES + t + 1)
                if t < 2:
                    pe.wait_ge(y_ok, 4 * n)
                if t == TILES:
                    pe.wait_ge(k_hi, n + 1)
                    pe.wait_ge(k_lo, n + 1)
                    pe.wait_ge(v_hi, n + 1)
                    pe.wait_ge(v_lo, n + 1)
                if t not in (TILES, TILES + 1):
                    wait(pe, f_scaled, t - 1)
                for i in range(KC):
                    for a in (HI, LO):
                        last = pe.matmul(ffn_bank(t)[:, :], xT[:, a, i, t * P:(t + 1) * P], ff_w[:, i, :],
                                         start=(i == 0 and a == HI), stop=(i == KC - 1 and a == LO))
                last.then_inc(f_mm, 1)

            pe.wait_ge(const_ok, 1)
            pe.wait_ge(seed_ok, 4)
            for _ in range(WARM_UP):
                pe.matmul(pp[:, :], ident[:, :], ident[:, :].unsqueeze(1).to_broadcast([P, BT // P, P]),
                          start=True, stop=True)
            for t in range(TILES):
                ln_transpose(t, 0)
            for h in range(HPG):
                q_unit(0, 0, 0, h, True)
            k_unit(0, 0, 0, True)
            v_unit(0, 0, 0, range(TILES))

            def step(g, tb, first, last):
                n = 4 * g + tb
                gm, tbm, m = following(g, tb)
                ahead = not (last and tb == BLOCKS - 1)
                in_first = first and tbm > 0
                ln = ln_tiles(tb, first, last)
                final = last and tb == BLOCKS - 1
                score_unit(n, 0)
                if final:
                    ffn_unit(0, n)
                    ffn_unit(1, n)
                if first and tb == 0:
                    for t in range(TILES, 2 * TILES):
                        ln_transpose(t, 0)
                if ahead:
                    q_unit(gm, tbm, m, 0, in_first)
                score_unit(n, 1)
                if final:
                    ffn_unit(2, n)
                    ffn_unit(3, n)
                    ffn_unit(4, n)
                if ahead:
                    q_unit(gm, tbm, m, 1, in_first)
                    q_unit(gm, tbm, m, 2, in_first)
                    q_unit(gm, tbm, m, 3, in_first)
                p_transpose(n, 0)
                if final:
                    ffn_unit(5, n)
                if ahead:
                    k_unit(gm, tbm, m, in_first)
                p_transpose(n, 1)
                if final:
                    ffn_unit(6, n)
                if ahead:
                    v_unit(gm, tbm, m, range(TILES // 2))
                if first and tb < 3:
                    pe.wait_ge(xT_ok, (tb + 2) * TILES)
                elif last and tb > 1:
                    pe.wait_ge(xT_ok, (BLOCKS + tb - 1) * TILES)
                av_unit(n, tb % 2, 0)
                if final:
                    ffn_unit(7, n)
                av_unit(n, tb % 2, 1)
                if ahead:
                    v_unit(gm, tbm, m, range(TILES // 2, TILES))
                if final:
                    pe.wait_ge(f_scaled, TILES)
                y_unit(g, n, 0)
                av_unit(n, tb % 2, 2)
                y_unit(g, n, 1)
                av_unit(n, tb % 2, 3)
                y_unit(g, n, 2)
                if ln is not None:
                    ln_transpose(ln, 4 * n + 4)
                    ln_transpose(ln + 1, 4 * n + 4)
                y_unit(g, n, 3)
                if ln is not None and not final:
                    ln_transpose(ln + 2, 4 * n + 4)
                    ln_transpose(ln + 3, 4 * n + 4)

            groups(pe, step)
            n = BLOCKS * GROUPS
            t0 = (BLOCKS - 1) * TILES
            for t in range(t0 - TILES, t0):
                if t - t0 + TILES < 2:
                    ln_transpose(BLOCKS * TILES + t + 2, 4 * n)
                ffn_unit(t, n)
            ln_transpose(BLOCKS * TILES + t0, 4 * n)
            for t in range(t0, t0 + TILES):
                if t + 1 < t0 + TILES:
                    ln_transpose(BLOCKS * TILES + t + 1, 4 * n)
                ffn_unit(t, n)


def kernel(**inputs):
    import numpy as np
    import concourse.bacc as bacc
    from concourse.bass_utils import run_bass_kernel_spmd

    a = {name: np.asarray(v) for name, v in inputs.items()}
    laid = {
        "x": a["x"].reshape(BLOCKS * TILES, P, D),
        "ctxT": a["ctx_4096"].reshape(BLOCKS, BT, KC, P).transpose(0, 3, 2, 1).reshape(BLOCKS, P, KC * BT),
        "wqT": a["L0_xattn_Wq"].reshape(GROUPS, HPG, DK, KC, P).transpose(0, 4, 1, 3, 2).reshape(GROUPS, P, HPG * KC * DK),
        "wkT": a["L0_xattn_Wk"].reshape(GROUPS, DK, KC, P).transpose(0, 3, 2, 1).reshape(GROUPS, P, KC * DK),
        "wvT": a["L0_xattn_Wv"].reshape(GROUPS, DK, KC, P).transpose(0, 3, 2, 1).reshape(GROUPS, P, KC * DK),
        "wdT": a["L0_xattn_Wd"].reshape(D, GROUPS, HPG, DK).transpose(1, 3, 2, 0).reshape(GROUPS, DK, HPG * D),
        "g_x": a["g_xattn"].reshape(1),
        "g_f": a["g_ffn"].reshape(1),
        "qw": a["L0_ffn_qweight"].reshape(D, P, 3).transpose(2, 1, 0),
        "w_scale": a["L0_ffn_weight_scale"].reshape(D),
        "w_zero": a["L0_ffn_weight_zero_point"].reshape(D),
        "bias": a["L0_ffn_bias"].reshape(D),
    }
    laid = {name: np.ascontiguousarray(v) for name, v in laid.items()}
    nc = bacc.Bacc("TRN2", target_bir_lowering=False, num_devices=1)
    args = [nc.dram_tensor(f"in_{name}", v.shape, mybir.dt.from_np(v.dtype), kind="ExternalInput").ap()
            for name, v in laid.items()]
    result = nc.dram_tensor("out_x", (BLOCKS * TILES, P, D), F32, kind="ExternalOutput").ap()
    build(nc, *args, result)
    r = run_bass_kernel_spmd(nc, [{f"in_{name}": v for name, v in laid.items()}], core_ids=[0])
    return r.results[0]["out_x"].reshape(B, S, D)
```
